# Optimizing a Trainium2 kernel written in Bass

```python
import numpy as np
import jax
import jax.numpy as jnp

def _softmax(x, axis=-1):
    return jax.nn.softmax(x, axis=axis)

def _gelu(x):
    return jax.nn.gelu(x, approximate=True)

def _silu(x):
    return jax.nn.silu(x)

def _sigmoid(x):
    return jax.nn.sigmoid(x)

def _layernorm(x, axis=-1, eps=1e-05):
    m = jnp.mean(x, axis=axis, keepdims=True)
    v = jnp.var(x, axis=axis, keepdims=True)
    return (x - m) / jnp.sqrt(v + eps)

def _scatter_add(tgt, idx, src, axis=0):
    return tgt.at[idx].add(src)

def _segment_sum(src, seg, n):
    return jax.ops.segment_sum(src, seg, n)
kernel_name = 'mk_perceiver_d1_seqx_r4_e68285'

def setup_inputs(seed: int=0):
    np.random.seed(seed)
    _w = jnp.asarray

    def _rec_inputs():
        import jax
        import jax.numpy as jnp
        _rk = jax.random.key(seed)
        x = -0.000125 + 0.9999 * jax.random.normal(jax.random.fold_in(_rk, 1), (1, 128, 512), jnp.float32)
        _lenS = 128 - jax.random.randint(jax.random.fold_in(_rk, 7), (1,), 0, max(1, 128 // 4) + 1, jnp.int32)
        _lenS2 = 12544 - jax.random.randint(jax.random.fold_in(_rk, 8), (1,), 0, max(1, 12544 // 4) + 1, jnp.int32)
        _ctx_2048P = jax.random.normal(jax.random.fold_in(_rk, 11), (1, 16, 512), jnp.float32)
        _ctx_2048c = jax.random.dirichlet(jax.random.fold_in(_rk, 511), 0.3 * jnp.ones((16,), jnp.float32), (1, 12544))
        _ctx_2048t = jnp.einsum('bsk,bkd->bsd', _ctx_2048c, _ctx_2048P)
        _ctx_2048t = _ctx_2048t * jax.lax.rsqrt(jnp.mean(jnp.square(_ctx_2048t)) + 1e-12) * 0.953939
        ctx_2048 = 1.72703e-05 + 1.00003 * (_ctx_2048t + 0.3 * jax.random.normal(jax.random.fold_in(_rk, 611), (1, 12544, 512), jnp.float32))
        return (x, ctx_2048)
    x, ctx_2048 = _rec_inputs()

    def _L0_xattn_setup():
        import jax, jax.numpy as jnp
        import numpy as np
        DIM = 512
        NH = 16
        HD = DIM // NH
        EPS = 1e-06
        IMG_LEN = 257

        def rms_norm(x, w, eps=EPS):
            xf = x.astype(jnp.float32)
            y = xf * jax.lax.rsqrt(jnp.mean(xf * xf, axis=-1, keepdims=True) + eps)
            return y.astype(x.dtype) * w

        def linear(x, w, b):
            return jnp.einsum('blc,oc->blo', x, w) + b

        def attention(q, k, v):
            scale = 1.0 / jnp.sqrt(jnp.asarray(HD, q.dtype))
            scores = jnp.einsum('bqhd,bkhd->bhqk', q, k) * scale
            probs = jax.nn.softmax(scores, axis=-1)
            return jnp.einsum('bhqk,bkhd->bqhd', probs, v)
        key = jax.random.key(seed)
        ks = jax.random.split(key, 12)
        B, L = (2, 2048)
        s = 0.02
        inp = {'x': jax.random.normal(ks[0], (B, L, DIM), jnp.float32), 'context': jax.random.normal(ks[1], (B, 769, DIM), jnp.float32), 'q_w': jax.random.normal(ks[2], (DIM, DIM), jnp.float32) * s, 'q_b': jnp.zeros((DIM,), jnp.float32), 'k_w': jax.random.normal(ks[3], (DIM, DIM), jnp.float32) * s, 'k_b': jnp.zeros((DIM,), jnp.float32), 'v_w': jax.random.normal(ks[4], (DIM, DIM), jnp.float32) * s, 'v_b': jnp.zeros((DIM,), jnp.float32), 'k_img_w': jax.random.normal(ks[5], (DIM, DIM), jnp.float32) * s, 'k_img_b': jnp.zeros((DIM,), jnp.float32), 'v_img_w': jax.random.normal(ks[6], (DIM, DIM), jnp.float32) * s, 'v_img_b': jnp.zeros((DIM,), jnp.float32), 'o_w': jax.random.normal(ks[7], (DIM, DIM), jnp.float32) * s, 'o_b': jnp.zeros((DIM,), jnp.float32), 'norm_q_w': jnp.ones((DIM,), jnp.float32), 'norm_k_w': jnp.ones((DIM,), jnp.float32), 'norm_k_img_w': jnp.ones((DIM,), jnp.float32)}
        return inp
    _L0_xattn_all = _L0_xattn_setup()
    _L0_xattn_in = {k: v for k, v in _L0_xattn_all.items() if k in ('q_w', 'q_b', 'k_w', 'k_b', 'v_w', 'v_b', 'k_img_w', 'k_img_b', 'v_img_w', 'v_img_b', 'o_w', 'o_b', 'norm_q_w', 'norm_k_w', 'norm_k_img_w')}
    del _L0_xattn_all

    def _L0_attn_setup():
        import jax, jax.numpy as jnp
        import numpy as np
        BLOCK = 32
        NUM_HEADS = 16
        HEAD_DIM = 128
        FP4_GRID = jnp.array([0.0, 0.5, 1.0, 1.5, 2.0, 3.0, 4.0, 6.0], dtype=jnp.float32)

        def quantize_to_mxfp4(w, block_size=BLOCK):
            D, F = w.shape
            blocks = w.reshape(D // block_size, block_size, F)
            amax = jnp.max(jnp.abs(blocks), axis=1)
            e = jnp.floor(jnp.log2(jnp.maximum(amax, 1e-12) / 6.0))
            scale = jnp.exp2(e)
            v = blocks / scale[:, None, :]
            idx = jnp.argmin(jnp.abs(jnp.abs(v)[..., None] - FP4_GRID), axis=-1)
            codes = jnp.sign(v) * FP4_GRID[idx]
            return (codes.reshape(D, F).astype(jnp.float32), scale.astype(jnp.float32))

        def _mxfp4_matmul(x, codes, scales, block_size=BLOCK):
            w = codes * jnp.repeat(scales, block_size, axis=0)
            return x @ w
        key = jax.random.key(seed)
        ks = jax.random.split(key, 9)
        B, S, D = (2, 512, 512)
        feat = NUM_HEADS * HEAD_DIM
        x = jax.random.normal(ks[0], (B, S, D), dtype=jnp.float32)

        def make_w(k, din, dout):
            w = jax.random.normal(k, (din, dout), dtype=jnp.float32) * (1.0 / np.sqrt(din))
            return quantize_to_mxfp4(w, BLOCK)
        wq_codes, wq_scales = make_w(ks[1], D, feat)
        wk_codes, wk_scales = make_w(ks[2], D, feat)
        wv_codes, wv_scales = make_w(ks[3], D, feat)
        wo_codes, wo_scales = make_w(ks[4], feat, D)
        bq = jnp.zeros((feat,), jnp.float32)
        bk = jnp.zeros((feat,), jnp.float32)
        bv = jnp.zeros((feat,), jnp.float32)
        bo = jnp.zeros((D,), jnp.float32)
        return {'x': x, 'wq_codes': wq_codes, 'wq_scales': wq_scales, 'bq': bq, 'wk_codes': wk_codes, 'wk_scales': wk_scales, 'bk': bk, 'wv_codes': wv_codes, 'wv_scales': wv_scales, 'bv': bv, 'wo_codes': wo_codes, 'wo_scales': wo_scales, 'bo': bo}
    _L0_attn_all = _L0_attn_setup()
    _L0_attn_in = {k: v for k, v in _L0_attn_all.items() if k in ('wq_codes', 'wq_scales', 'bq', 'wk_codes', 'wk_scales', 'bk', 'wv_codes', 'wv_scales', 'bv', 'wo_codes', 'wo_scales', 'bo')}
    del _L0_attn_all

    def _L0_ffn_setup():
        import jax, jax.numpy as jnp
        import numpy as np
        E = 32
        K = 4
        G = 4
        TG = 2
        H = 512
        F = 256
        FS = 512
        SCALE = 2.0
        B, S = (2, 256)
        N = B * S
        CAP = 2 * (N * K // E)

        def _gate(x, gate_w, gate_bias):
            logits = x @ gate_w.T
            scores = jax.nn.sigmoid(logits)
            sc = scores + gate_bias
            n = x.shape[0]
            grp = sc.reshape(n, G, E // G)
            group_scores = jax.lax.top_k(grp, 2)[0].sum(-1)
            _, gidx = jax.lax.top_k(group_scores, TG)
            gmask = jnp.zeros((n, G), sc.dtype).at[jnp.arange(n)[:, None], gidx].set(1.0)
            smask = jnp.repeat(gmask, E // G, axis=1)
            tmp = jnp.where(smask > 0, sc, 0.0)
            _, topk_idx = jax.lax.top_k(tmp, K)
            topk_w = jnp.take_along_axis(scores, topk_idx, axis=1)
            topk_w = topk_w / (topk_w.sum(-1, keepdims=True) + 1e-20)
            return (topk_idx, topk_w * SCALE)

        def _moe(x, topk_idx, topk_w, w1, w2, w3):
            n = x.shape[0]
            flat_e = topk_idx.reshape(-1)
            oh = jax.nn.one_hot(flat_e, E, dtype=jnp.int32)
            pos = (jnp.cumsum(oh, axis=0) * oh).sum(-1) - 1
            keep = pos < CAP
            slot = jnp.where(keep, pos, CAP)
            x_rep = jnp.repeat(x, K, axis=0)
            buf = jnp.zeros((E, CAP, H), x.dtype).at[flat_e, slot].set(x_rep, mode='drop')
            h = jax.nn.silu(jnp.einsum('ech,ehf->ecf', buf, w1)) * jnp.einsum('ech,ehf->ecf', buf, w3)
            ob = jnp.einsum('ecf,efh->ech', h, w2)
            y = ob[flat_e, jnp.minimum(slot, CAP - 1)]
            y = jnp.where(keep[:, None], y, 0.0)
            return (y.reshape(n, K, H) * topk_w[:, :, None]).sum(1)
        key = jax.random.key(seed)
        ks = jax.random.split(key, 9)
        w = 0.02
        return {'hidden_states': jax.random.normal(ks[0], (B, S, H), jnp.float32), 'gate_w': jax.random.normal(ks[1], (E, H), jnp.float32) * w, 'gate_bias': jax.random.normal(ks[2], (E,), jnp.float32) * w, 'w1': jax.random.normal(ks[3], (E, H, F), jnp.float32) * w, 'w2': jax.random.normal(ks[4], (E, F, H), jnp.float32) * w, 'w3': jax.random.normal(ks[5], (E, H, F), jnp.float32) * w, 'shared_gate': jax.random.normal(ks[6], (H, FS), jnp.float32) * w, 'shared_up': jax.random.normal(ks[7], (H, FS), jnp.float32) * w, 'shared_down': jax.random.normal(ks[8], (FS, H), jnp.float32) * w}
    _L0_ffn_all = _L0_ffn_setup()
    _L0_ffn_in = {k: v for k, v in _L0_ffn_all.items() if k in ('gate_w', 'gate_bias', 'w1', 'w2', 'w3', 'shared_gate', 'shared_up', 'shared_down')}
    del _L0_ffn_all
    return {'x': x, 'ctx_2048': ctx_2048, 'L0_xattn_q_w': _L0_xattn_in['q_w'], 'L0_xattn_q_b': _L0_xattn_in['q_b'], 'L0_xattn_k_w': _L0_xattn_in['k_w'], 'L0_xattn_k_b': _L0_xattn_in['k_b'], 'L0_xattn_v_w': _L0_xattn_in['v_w'], 'L0_xattn_v_b': _L0_xattn_in['v_b'], 'L0_xattn_k_img_w': _L0_xattn_in['k_img_w'], 'L0_xattn_k_img_b': _L0_xattn_in['k_img_b'], 'L0_xattn_v_img_w': _L0_xattn_in['v_img_w'], 'L0_xattn_v_img_b': _L0_xattn_in['v_img_b'], 'L0_xattn_o_w': _L0_xattn_in['o_w'], 'L0_xattn_o_b': _L0_xattn_in['o_b'], 'L0_xattn_norm_q_w': _L0_xattn_in['norm_q_w'], 'L0_xattn_norm_k_w': _L0_xattn_in['norm_k_w'], 'L0_xattn_norm_k_img_w': _L0_xattn_in['norm_k_img_w'], 'L0_attn_wq_codes': _L0_attn_in['wq_codes'], 'L0_attn_wq_scales': _L0_attn_in['wq_scales'], 'L0_attn_bq': _L0_attn_in['bq'], 'L0_attn_wk_codes': _L0_attn_in['wk_codes'], 'L0_attn_wk_scales': _L0_attn_in['wk_scales'], 'L0_attn_bk': _L0_attn_in['bk'], 'L0_attn_wv_codes': _L0_attn_in['wv_codes'], 'L0_attn_wv_scales': _L0_attn_in['wv_scales'], 'L0_attn_bv': _L0_attn_in['bv'], 'L0_attn_wo_codes': _L0_attn_in['wo_codes'], 'L0_attn_wo_scales': _L0_attn_in['wo_scales'], 'L0_attn_bo': _L0_attn_in['bo'], 'L0_ffn_gate_w': _L0_ffn_in['gate_w'], 'L0_ffn_gate_bias': _L0_ffn_in['gate_bias'], 'L0_ffn_w1': _L0_ffn_in['w1'], 'L0_ffn_w2': _L0_ffn_in['w2'], 'L0_ffn_w3': _L0_ffn_in['w3'], 'L0_ffn_shared_gate': _L0_ffn_in['shared_gate'], 'L0_ffn_shared_up': _L0_ffn_in['shared_up'], 'L0_ffn_shared_down': _L0_ffn_in['shared_down']}

def reference(x, ctx_2048, L0_xattn_q_w, L0_xattn_q_b, L0_xattn_k_w, L0_xattn_k_b, L0_xattn_v_w, L0_xattn_v_b, L0_xattn_k_img_w, L0_xattn_k_img_b, L0_xattn_v_img_w, L0_xattn_v_img_b, L0_xattn_o_w, L0_xattn_o_b, L0_xattn_norm_q_w, L0_xattn_norm_k_w, L0_xattn_norm_k_img_w, L0_attn_wq_codes, L0_attn_wq_scales, L0_attn_bq, L0_attn_wk_codes, L0_attn_wk_scales, L0_attn_bk, L0_attn_wv_codes, L0_attn_wv_scales, L0_attn_bv, L0_attn_wo_codes, L0_attn_wo_scales, L0_attn_bo, L0_ffn_gate_w, L0_ffn_gate_bias, L0_ffn_w1, L0_ffn_w2, L0_ffn_w3, L0_ffn_shared_gate, L0_ffn_shared_up, L0_ffn_shared_down):
    import jax
    import jax.numpy as jnp

    def _L0_xattn_ref(x, context, q_w, q_b, k_w, k_b, v_w, v_b, k_img_w, k_img_b, v_img_w, v_img_b, o_w, o_b, norm_q_w, norm_k_w, norm_k_img_w):
        import jax, jax.numpy as jnp
        import numpy as np
        DIM = 512
        NH = 16
        HD = DIM // NH
        EPS = 1e-06
        IMG_LEN = 257

        def rms_norm(x, w, eps=EPS):
            xf = x.astype(jnp.float32)
            y = xf * jax.lax.rsqrt(jnp.mean(xf * xf, axis=-1, keepdims=True) + eps)
            return y.astype(x.dtype) * w

        def linear(x, w, b):
            return jnp.einsum('blc,oc->blo', x, w) + b

        def attention(q, k, v):
            scale = 1.0 / jnp.sqrt(jnp.asarray(HD, q.dtype))
            scores = jnp.einsum('bqhd,bkhd->bhqk', q, k) * scale
            probs = jax.nn.softmax(scores, axis=-1)
            return jnp.einsum('bhqk,bkhd->bqhd', probs, v)
        B, L, _ = x.shape
        ctx_img = context[:, :IMG_LEN]
        ctx_txt = context[:, IMG_LEN:]
        q = rms_norm(linear(x, q_w, q_b), norm_q_w).reshape(B, L, NH, HD)
        k = rms_norm(linear(ctx_txt, k_w, k_b), norm_k_w).reshape(B, -1, NH, HD)
        v = linear(ctx_txt, v_w, v_b).reshape(B, -1, NH, HD)
        k_img = rms_norm(linear(ctx_img, k_img_w, k_img_b), norm_k_img_w).reshape(B, -1, NH, HD)
        v_img = linear(ctx_img, v_img_w, v_img_b).reshape(B, -1, NH, HD)
        img_x = attention(q, k_img, v_img)
        txt_x = attention(q, k, v)
        out = (txt_x + img_x).reshape(B, L, DIM)
        return linear(out, o_w, o_b)

    def _L0_attn_ref(x, wq_codes, wq_scales, bq, wk_codes, wk_scales, bk, wv_codes, wv_scales, bv, wo_codes, wo_scales, bo):
        import jax, jax.numpy as jnp
        import numpy as np
        BLOCK = 32
        NUM_HEADS = 16
        HEAD_DIM = 128
        FP4_GRID = jnp.array([0.0, 0.5, 1.0, 1.5, 2.0, 3.0, 4.0, 6.0], dtype=jnp.float32)

        def quantize_to_mxfp4(w, block_size=BLOCK):
            D, F = w.shape
            blocks = w.reshape(D // block_size, block_size, F)
            amax = jnp.max(jnp.abs(blocks), axis=1)
            e = jnp.floor(jnp.log2(jnp.maximum(amax, 1e-12) / 6.0))
            scale = jnp.exp2(e)
            v = blocks / scale[:, None, :]
            idx = jnp.argmin(jnp.abs(jnp.abs(v)[..., None] - FP4_GRID), axis=-1)
            codes = jnp.sign(v) * FP4_GRID[idx]
            return (codes.reshape(D, F).astype(jnp.float32), scale.astype(jnp.float32))

        def _mxfp4_matmul(x, codes, scales, block_size=BLOCK):
            w = codes * jnp.repeat(scales, block_size, axis=0)
            return x @ w
        B, S, D = x.shape
        q = _mxfp4_matmul(x, wq_codes, wq_scales) + bq
        k = _mxfp4_matmul(x, wk_codes, wk_scales) + bk
        v = _mxfp4_matmul(x, wv_codes, wv_scales) + bv
        q = q.reshape(B, S, NUM_HEADS, HEAD_DIM)
        k = k.reshape(B, S, NUM_HEADS, HEAD_DIM)
        v = v.reshape(B, S, NUM_HEADS, HEAD_DIM)
        scores = jnp.einsum('bqhd,bkhd->bhqk', q, k) / jnp.sqrt(jnp.float32(HEAD_DIM))
        attn = jax.nn.softmax(scores, axis=-1)
        out = jnp.einsum('bhqk,bkhd->bqhd', attn, v).reshape(B, S, NUM_HEADS * HEAD_DIM)
        return _mxfp4_matmul(out, wo_codes, wo_scales) + bo

    def _L0_ffn_ref(hidden_states, gate_w, gate_bias, w1, w2, w3, shared_gate, shared_up, shared_down):
        import jax, jax.numpy as jnp
        import numpy as np
        E = 32
        K = 4
        G = 4
        TG = 2
        H = 512
        F = 256
        FS = 512
        SCALE = 2.0
        B, S = (2, 256)
        N = B * S
        CAP = 2 * (N * K // E)

        def _gate(x, gate_w, gate_bias):
            logits = x @ gate_w.T
            scores = jax.nn.sigmoid(logits)
            sc = scores + gate_bias
            n = x.shape[0]
            grp = sc.reshape(n, G, E // G)
            group_scores = jax.lax.top_k(grp, 2)[0].sum(-1)
            _, gidx = jax.lax.top_k(group_scores, TG)
            gmask = jnp.zeros((n, G), sc.dtype).at[jnp.arange(n)[:, None], gidx].set(1.0)
            smask = jnp.repeat(gmask, E // G, axis=1)
            tmp = jnp.where(smask > 0, sc, 0.0)
            _, topk_idx = jax.lax.top_k(tmp, K)
            topk_w = jnp.take_along_axis(scores, topk_idx, axis=1)
            topk_w = topk_w / (topk_w.sum(-1, keepdims=True) + 1e-20)
            return (topk_idx, topk_w * SCALE)

        def _moe(x, topk_idx, topk_w, w1, w2, w3):
            n = x.shape[0]
            flat_e = topk_idx.reshape(-1)
            oh = jax.nn.one_hot(flat_e, E, dtype=jnp.int32)
            pos = (jnp.cumsum(oh, axis=0) * oh).sum(-1) - 1
            keep = pos < CAP
            slot = jnp.where(keep, pos, CAP)
            x_rep = jnp.repeat(x, K, axis=0)
            buf = jnp.zeros((E, CAP, H), x.dtype).at[flat_e, slot].set(x_rep, mode='drop')
            h = jax.nn.silu(jnp.einsum('ech,ehf->ecf', buf, w1)) * jnp.einsum('ech,ehf->ecf', buf, w3)
            ob = jnp.einsum('ecf,efh->ech', h, w2)
            y = ob[flat_e, jnp.minimum(slot, CAP - 1)]
            y = jnp.where(keep[:, None], y, 0.0)
            return (y.reshape(n, K, H) * topk_w[:, :, None]).sum(1)
        b, s, h = hidden_states.shape
        x = hidden_states.reshape(-1, h)
        topk_idx, topk_w = _gate(x, gate_w, gate_bias)
        out = _moe(x, topk_idx, topk_w, w1, w2, w3)
        shared = jax.nn.silu(x @ shared_gate) * (x @ shared_up) @ shared_down
        return (out + shared).reshape(b, s, h)
    x = x + _L0_xattn_ref(_layernorm(x, axis=-1), ctx_2048, L0_xattn_q_w, L0_xattn_q_b, L0_xattn_k_w, L0_xattn_k_b, L0_xattn_v_w, L0_xattn_v_b, L0_xattn_k_img_w, L0_xattn_k_img_b, L0_xattn_v_img_w, L0_xattn_v_img_b, L0_xattn_o_w, L0_xattn_o_b, L0_xattn_norm_q_w, L0_xattn_norm_k_w, L0_xattn_norm_k_img_w)
    x = x + _L0_attn_ref(_layernorm(x, axis=-1), L0_attn_wq_codes, L0_attn_wq_scales, L0_attn_bq, L0_attn_wk_codes, L0_attn_wk_scales, L0_attn_bk, L0_attn_wv_codes, L0_attn_wv_scales, L0_attn_bv, L0_attn_wo_codes, L0_attn_wo_scales, L0_attn_bo)
    x = x + _L0_ffn_ref(_layernorm(x, axis=-1), L0_ffn_gate_w, L0_ffn_gate_bias, L0_ffn_w1, L0_ffn_w2, L0_ffn_w3, L0_ffn_shared_gate, L0_ffn_shared_up, L0_ffn_shared_down)
    return x

_drawn_inputs = setup_inputs


def setup_inputs(seed=0):
    import zlib

    import numpy as np

    out = dict(_drawn_inputs(seed))
    spreads = {'L0_xattn_q_b': (0.0, 0.504),
     'L0_xattn_k_b': (0.0, 0.8),
     'L0_xattn_v_b': (0.0, 0.1),
     'L0_xattn_k_img_b': (0.0, 0.8),
     'L0_xattn_v_img_b': (0.0, 0.1),
     'L0_xattn_o_b': (0.0, 0.1),
     'L0_xattn_norm_q_w': (1.0, 0.6),
     'L0_xattn_norm_k_w': (1.0, 0.6),
     'L0_xattn_norm_k_img_w': (1.0, 0.6),
     'L0_attn_bq': (0.0, 0.754),
     'L0_attn_bk': (0.0, 0.8),
     'L0_attn_bv': (0.0, 0.1),
     'L0_attn_bo': (0.0, 0.1)}
    factors = {'L0_ffn_gate_bias': 3.908}
    for name, (base, spread) in spreads.items():
        noise = np.random.default_rng([zlib.crc32(name.encode()), seed]).standard_normal(out[name].shape)
        drawn = base * np.exp(spread * noise) if base else spread * noise
        out[name] = jnp.asarray(drawn.astype(out[name].dtype))
    for name, factor in factors.items():
        out[name] = (out[name] * factor).astype(out[name].dtype)
    return out
```

```python
import concourse.bass as bass
from concourse import mybir
from contextlib import ExitStack

F32 = mybir.dt.float32
F32R = mybir.dt.float32r
ALU = mybir.AluOpType
ACT = mybir.ActivationFunctionType
AX = mybir.AxisListType

P = 128
D = 512
DC = D // P
NH, HD = 16, 32
HC = P // HD
NK = 12544
IMG = 257
GK = 512
GT = GK // P
TXT0 = IMG - 1
NG = 1 + (NK - TXT0) // GK
assert TXT0 + (NG - 1) * GK == NK and IMG <= GK
SH, SD = 16, 128
SF = SH * SD
HB = 4
NB = SH // HB
QB = 32
NE, NF = 32, 256
NGRP, TOPG, TOPK = 4, 2, 4
GE = NE // NGRP
FS = 512
RSCALE = 2.0
BIG = 3.0e38
LN_EPS, RMS_EPS = 1e-5, 1e-6


class Event:

    def __init__(self, sem, per=0, by=1):
        self.sem, self.per, self.by, self.n = sem, per, by, 0

    def done(self, ins):
        ins.then_inc(self.sem, self.by)
        self.n += 1
        return self.n

    def part(self, ins):
        ins.then_inc(self.sem, 16)

    def wait(self, eng, rnd, n):
        eng.wait_ge(self.sem, (rnd * self.per + n) * self.by)


def program(nc, t, out):
    ctx = ExitStack()
    with ctx:
        base = (nc.sbuf_base + 31) // 32 * 32
        KB = 1024
        ctx.enter_context(nc.sbuf_tensor("arena", [P, 207 * KB // 4 + 128], F32))

        def sb(name, off, shape, dt=F32):
            return nc.alloc_sbuf_tensor_at(name, shape, dt, offset=base + off)

        def event(name, per=0, by=1):
            return Event(ctx.enter_context(nc.semaphore(name)), per, by)

        W_NAMES = ["k_img", "v_img", "k", "v"]
        w_hi = [sb(f"w_hi_{n}", 16 * i * KB, [P, DC, D], F32R) for i, n in enumerate(W_NAMES)]
        w_lo = [sb(f"w_lo_{n}", (16 * i + 8) * KB, [P, DC, D], F32R) for i, n in enumerate(W_NAMES)]
        qz_hi = [sb(f"qz_hi{i}", (64 + 16 * i) * KB, [P, NH, P], F32R) for i in range(2)]
        qz_lo = [sb(f"qz_lo{i}", (72 + 16 * i) * KB, [P, NH, P], F32R) for i in range(2)]
        kt_hi = [sb(f"kt_hi{i}", (96 + 16 * i) * KB, [P, DC, GK], F32R) for i in range(2)]
        kt_lo = [sb(f"kt_lo{i}", (104 + 16 * i) * KB, [P, DC, GK], F32R) for i in range(2)]
        stage = [sb(f"stage{i}", (96 + 8 * i) * KB, [P, DC, D]) for i in range(4)]
        v_sb = [sb(f"v_sb{i}", (128 + 8 * i) * KB, [P, GT, D]) for i in range(2)]
        wq = sb("wq", 128 * KB, [P, DC, D])
        q_rows = sb("q_rows", 136 * KB, [P, 4, D])
        cx = [sb(f"cx{i}", (144 + 8 * i) * KB, [P, DC, GK]) for i in range(2)]
        cx_hi = [sb(f"cx_hi{i}", (160 + 2 * i) * KB, [P, DC, P], F32R) for i in range(2)]
        cx_lo = [sb(f"cx_lo{i}", (164 + 2 * i) * KB, [P, DC, P], F32R) for i in range(2)]
        kb = [sb(f"kb{i}", (168 + 2 * i) * KB, [P, D]) for i in range(2)]
        kn = [sb(f"kn{i}", (172 + 2 * i) * KB, [P, D]) for i in range(2)]
        NP = 4
        p_sb = [sb(f"p{i}", o, [P, GK]) for i, o in enumerate((176 * KB, 178 * KB, 180 * KB, 205 * KB + 512))]
        pt_sb = [sb(f"pt{i}", (182 + 2 * i) * KB, [P, GK]) for i in range(2)]
        k_bias = sb("k_bias", 186 * KB, [P, 2, D])
        ot_sb = sb("ot_sb", 190 * KB, [P, D])
        o_st = [sb(f"o_st{i}", (192 + 2 * i) * KB, [P, D]) for i in range(2)]
        x_sb = sb("x_sb", 196 * KB, [P, D])
        o_rows = sb("o_rows", 198 * KB, [P, 3, D])
        ident = sb("ident", 204 * KB, [P, P])
        small = sb("small", 204 * KB + 512, [P, 256])
        cols = iter(range(0, 256, 16))
        nm = [small[:, c:c + NH] for c in (next(cols), next(cols))]
        nm_init, ngm, dm, al = (small[:, c:c + NH] for c in (next(cols), next(cols), next(cols), next(cols)))
        ls = [small[:, c:c + NH] for c in (next(cols), next(cols))]
        l_st = [small[:, c:c + NH] for c in (next(cols), next(cols))]
        c = next(cols)
        k_ss, k_r = small[:, c:c + GT], small[:, c + GT:c + 2 * GT]
        c = next(cols)
        stats, mv, rstd, q_ss, q_r = (small[:, c:c + 6], small[:, c + 6:c + 8], small[:, c + 8:c + 9],
                                      small[:, c + 9:c + 10], small[:, c + 10:c + 11])
        rl = small[:, 192:192 + NH]
        zero_col, ln_eps, rms_eps, minus_half = (small[:, i:i + 1] for i in range(208, 212))
        one_col = small[:, 221:222]
        k_t, r_t = small[:, 212:212 + GT], small[:, 220:221]
        wo = sb("wo", 64 * KB, [P, DC, D])
        xn, xnt, qf, qn = kb[0], kb[1], kn[0], kn[1]

        codes = [sb(f"codes_{n}", 32 * i * KB, [P, DC, SF]) for i, n in enumerate("qkv")]
        codes_o = sb("codes_o", 96 * KB, [P, SH, D])
        NRING = 3
        ring = [sb(f"scale_ring{i}", (128 + 8 * i) * KB, [P, SF]) for i in range(NRING)]
        sv = sb("sv", 152 * KB, [P, SF])
        sq = sb("sq", 160 * KB, [P, SF])
        sqt = sb("sqt", 168 * KB, [P, SF])
        sk = sb("sk", 176 * KB, [P, SF])
        skt = sb("skt", 184 * KB, [P, SF])
        sp, spt, sot = sq, sk, skt
        bo_row = sb("bo_row", 192 * KB, [P, D])
        x1 = sb("x1", 194 * KB, [P, D])
        yn, ynt = sb("yn", 198 * KB, [P, D]), sb("ynt", 200 * KB, [P, D])
        s_max, s_nb, s_sum, s_rec = (small[:, i:i + SH] for i in (0, 16, 32, 48))

        NR = 8
        w13 = [sb(f"w13_{i}", 12 * i * KB, [P, DC, 2 * NF]) for i in range(NR)]
        w2 = [sb(f"w2_{i}", (12 * i + 8) * KB, [P, NF // P, D]) for i in range(NR)]
        sh_w = [sb(f"shared_{n}", (128 + 8 * i) * KB, [P, DC, FS]) for i, n in enumerate(["gate", "up", "down"])]
        earlier = sb("earlier", 152 * KB, [P, NE, NE])
        gate_w = sb("gate_w", 156 * KB, [P, DC, NE])
        gate_b = sb("gate_b", 156 * KB + 512, [P, NE])
        cmp_a = sb("cmp_a", 160 * KB, [P, NE, NE])
        cmp_b = sb("cmp_b", 164 * KB, [P, NE, NE])
        rt = sb("router", 168 * KB, [P, 16, NE])
        sh_e, sh_a = sb("sh_e", 170 * KB, [P, FS]), sb("sh_a", 172 * KB, [P, FS])
        sh_h, sh_ht = sb("sh_h", 174 * KB, [P, FS]), sb("sh_ht", 176 * KB, [P, FS])
        m_e = [sb(f"m_e{i}", (178 + i) * KB, [P, NF]) for i in range(2)]
        m_h = [sb(f"m_h{i}", (180 + i) * KB, [P, NF]) for i in range(2)]
        m_ht = [sb(f"m_ht{i}", (182 + i) * KB, [P, NF]) for i in range(2)]
        g_col = sb("g_col", 184 * KB, [P, NR])
        x2 = sb("x2", 186 * KB, [P, D])
        x3, x3t = sb("x3", 188 * KB, [P, D]), sb("x3t", 190 * KB, [P, D])
        y_out = sb("y_out", 202 * KB, [P, D])
        score, sc, tmp, sel, gw, rank = (rt[:, i, :] for i in range(6))
        top8 = rt[:, 8, :].rearrange("p (g e) -> p g e", g=NGRP)
        gs, gmask, grank = (rt[:, 9 + i, 0:NGRP] for i in range(3))
        wsum, wrec = rt[:, 14, 0:1], rt[:, 15, 0:1]

        ps = [ctx.enter_context(nc.psum_tensor(f"ps{i}", [P, 512], F32)) for i in range(8)]
        ps_k, ps_v, ps_t, ps_pt, ps_o = ps[0], ps[1], ps[2], ps[3], ps[4]
        ps_s = ps[5:7]
        NS = len(ps_s)

        e_x = event("x_loaded", by=16)
        e_wq = event("wq_loaded", by=16)
        e_rows = event("rows_loaded", by=16)
        e_w = [event(f"w_loaded_{n}", by=16) for n in W_NAMES]
        e_pool = event("pool_init")
        e_dve, e_act, e_pe = event("dve_chain"), event("act_chain"), event("pe_chain")
        e_whi, e_wlo = event("w_hi_split"), event("w_lo_split")
        e_cx = event("cx_loaded", 1, 16)
        e_chi, e_clo = event("cx_hi", GT), event("cx_lo", GT)
        e_kp, e_vp = event("k_projected", GT), event("v_projected", GT)
        e_kb, e_sq, e_r, e_kn = event("k_biased", GT), event("k_squared", GT), event("k_rms", GT), event("k_normed", GT)
        e_kt, e_khi, e_klo, e_v = event("k_transposed", GT), event("kt_hi", GT), event("kt_lo", GT), event("v_stored", GT)
        e_qk = event("scores", NH)
        e_gm, e_nm, e_exp = event("group_max", NH), event("running_max", NH), event("exp", NH)
        e_pt, e_pte, e_pv = event("p_transposed", NH), event("pt_stored", NH), event("pv", NH)
        e_dm, e_al, e_l1, e_l2 = event("max_step", 1), event("alpha", 1), event("l_scaled", 1), event("l_added", 1)
        e_osc, e_oc, e_ot, e_oadd = event("o_scaled", 1), event("ot_stored", 1), event("o_transposed", 1), event("o_added", 1)
        e_mask = event("masked", 1)
        e_wo = event("wo_loaded", by=16)
        e_osum, e_x1 = event("attention_summed"), event("x_after_cross")
        e_var, e_rs, e_rt = event("variance"), event("rsqrt"), event("k_mean_square", GT)
        e_out = event("out_stored", by=16)
        e_codes = [event(f"codes_loaded_{n}", by=16) for n in "qkvo"]
        e_ring = [event(f"ring_loaded{i}", by=16 * P // QB) for i in range(NRING)]
        e_bo, e_deq = event("bo_loaded", by=16), event("dequantised")
        e_ln, e_lnt, e_lntc = event("normed"), event("normed_t"), event("normed_t_stored")
        e_pj, e_pjb = event("self_projected"), event("self_biased")
        e_tr, e_trc = event("self_transposed"), event("self_transposed_stored")
        e_ss, e_smax, e_sexp, e_sn = event("self_scores"), event("self_max"), event("self_exp"), event("self_normed")
        e_spt, e_sptc = event("self_p_transposed"), event("self_p_stored")
        e_so, e_soc = event("self_out"), event("self_out_stored")
        e_sf, e_x2 = event("self_final"), event("x_after_self")
        e_shw, e_gate = event("shared_loaded", by=16), event("gate_loaded", by=16)
        e_ew = [event(f"expert_loaded{i}", 1, 48) for i in range(NR)]
        e_lg, e_lge, e_gw = event("logits"), event("logits_exp"), event("gate_weights")
        e_tri = event("earlier_made")
        e_sg, e_sge, e_shh, e_sht, e_shtc = (event(n) for n in ("shared_h", "shared_exp", "shared_hidden",
                                                               "shared_t", "shared_t_stored"))
        e_h, e_he, e_hid, e_ht, e_htc, e_y = (event(n, NR) for n in ("expert_h", "expert_exp", "expert_hidden",
                                                                    "expert_t", "expert_t_stored", "expert_y"))
        e_gc = event("gate_columns", 1)
        e_m1, e_m2, e_m3 = (event(n, NR) for n in ("expert_exp_plus1", "expert_sigmoid", "expert_gate"))
        e_yd, e_fin = event("y_done"), event("finished")

        ps_pj, ps_tr, ps_sc = ps[0:2], ps[2:4], ps[4:8]
        ps_lg, ps_sg, ps_su, ps_y, ps_h, ps_ht = ps[0], ps[1], ps[3], ps[4], ps[5:7], (ps[7], ps[2])

        def rows_of(ap):
            return ap.partition_broadcast(P)

        cxt = t["ctx_t"].rearrange("(c p) k -> p c k", p=P)

        def wview(ap):
            return ap.rearrange("(c p) o -> p c o", p=P)

        def steps(eng, step):
            step(eng, 0, 0)
            step(eng, 1, 1)
            step(eng, 2, 0)
            with eng.Fori(0, (NG - 3) // 2) as i:
                step(eng, i * 2 + 3, 1, loop=True)
                step(eng, i * 2 + 4, 0, loop=True)
            step(eng, NG, NG % 2)
            step(eng, NG + 1, (NG + 1) % 2)

        def parts(s, loop):
            return (loop or s < NG), (loop or 1 <= s <= NG), (loop or s >= 2)

        def mask(s, loop):
            if not loop and s == 1:
                return 0, IMG
            if not loop and s == 2:
                return 1, GK
            return 0, GK

        N_POOL = 2 + NP + 2 + 4 + 1 + 1 + 2 + 4
        block = ctx.enter_context(nc.Block())

        def ring_free(eng, item):
            old = item - NRING
            if old < 0:
                return
            i, c = divmod(old, DC + 1)
            if i < 3 and c == DC:
                e_pjb.wait(eng, 0, NB * (i + 1))
            elif i < 3:
                e_deq.wait(eng, 0, i * DC + c + 1)
            else:
                e_deq.wait(eng, 0, 3 * DC + old - 3 * (DC + 1) + 1)

        def ring_loaded(eng, item):
            e_ring[item % NRING].wait(eng, 0, item // NRING + 1)
            return ring[item % NRING]

        @block.sync
        def _(eng):
            e_x.done(eng.dma_start(x_sb[:, :], t["x"]))
            e_wq.done(eng.dma_start(wq[:, :, :], wview(t["q_wt"])))
            for i, n in enumerate(["q_b", "norm_q_w", "norm_k_img_w", "norm_k_w"]):
                e_rows.done(eng.dma_start(q_rows[:, i, :], rows_of(t[n])))
            for i, n in enumerate(["k_img_b", "k_b"]):
                e_rows.done(eng.dma_start(k_bias[:, i, :], rows_of(t[n])))
            for i, n in enumerate(["o_b", "v_b", "v_img_b"]):
                e_rows.done(eng.dma_start(o_rows[:, i, :], rows_of(t[n])))
            for i, n in enumerate(W_NAMES):
                e_w[i].done(eng.dma_start(stage[i][:, :, :], wview(t[n + "_wt"])))

            def load(g, par):
                if not (isinstance(g, int) and g < 2):
                    e_clo.wait(eng, g - 2, GT)
                    e_cx.wait(eng, g, 0)
                if isinstance(g, int) and g == 0:
                    src = cxt[:, :, 0:GK]
                elif isinstance(g, int):
                    src = cxt[:, :, TXT0 + (g - 1) * GK:TXT0 + g * GK]
                else:
                    src = cxt[:, :, bass.ds(g * GK + (TXT0 - GK), GK)]
                e_cx.done(eng.dma_start(cx[par][:, :, :], src))

            load(0, 0)
            e_cx.wait(eng, 1, 0)
            load(1, 1)
            load(2, 0)
            e_qk.wait(eng, 0, NH)
            e_wo.done(eng.dma_start(wo[:, :, :], wview(t["o_wt"])))
            with eng.Fori(0, (NG - 3) // 2) as i:
                load(i * 2 + 3, 1)
                load(i * 2 + 4, 0)
            e_x1.wait(eng, 0, 1)
            blocks = range(P // QB)
            for i, n in enumerate("qkv"):
                e_codes[i].done(eng.dma_start(codes[i][:, :, :], t[f"w{n}_codes"].rearrange("(c p) f -> p c f", p=P)))
                for c in range(DC):
                    item = i * (DC + 1) + c
                    ring_free(eng, item)
                    for b in blocks:
                        e_ring[item % NRING].part(eng.dma_start(
                            ring[item % NRING][b * QB:(b + 1) * QB, :],
                            t[f"w{n}_scales"][c * len(blocks) + b, :].partition_broadcast(QB)))
                item += 1
                ring_free(eng, item)
                for b in blocks:
                    e_ring[item % NRING].part(eng.dma_start(ring[item % NRING][b * QB:(b + 1) * QB, :],
                                                            t[f"b{n}"].partition_broadcast(QB)))
            e_codes[3].done(eng.dma_start(codes_o[:, :, :], t["wo_codes"].rearrange("(c p) f -> p c f", p=P)))
            so = t["wo_scales"].rearrange("(c b) f -> b c f", b=len(blocks))
            for k in range(NB):
                item = 3 * (DC + 1) + k
                ring_free(eng, item)
                for b in blocks:
                    e_ring[item % NRING].part(eng.dma_start(
                        ring[item % NRING][b * QB:(b + 1) * QB, :].rearrange("p (c f) -> p c f", c=HB),
                        so[b, k * HB:(k + 1) * HB, :].partition_broadcast(QB)))
            e_bo.done(eng.dma_start(bo_row[:, :], rows_of(t["bo"])))

            def load_expert(e, i):
                one = slice(e, e + 1) if isinstance(e, int) else bass.ds(e, 1)
                for half, n in enumerate(("w1", "w3")):
                    e_ew[i].part(eng.dma_start(w13[i][:, :, half * NF:(half + 1) * NF],
                                               t[n][one, :, :].rearrange("o (c p) f -> p (o c) f", p=P)))
                e_ew[i].part(eng.dma_start(w2[i][:, :, :], t["w2"][one, :, :].rearrange("o (c p) f -> p (o c) f", p=P)))

            for i in range(NR):
                last = ((i + 1) * 12 - 1) // 32
                e_pj.wait(eng, 0, NB * (last + 1))
                load_expert(i, i)
            e_deq.wait(eng, 0, 3 * DC + NB)
            for i, n in enumerate(("gate", "up", "down")):
                e_shw.done(eng.dma_start(sh_w[i][:, :, :], t[f"shared_{n}"].rearrange("(c p) f -> p c f", p=P)))
            e_so.wait(eng, 0, NB)
            e_gate.done(eng.dma_start(gate_w[:, :, :], t["gate_wt"].rearrange("(c p) f -> p c f", p=P)))
            e_gate.done(eng.dma_start(gate_b[:, :], rows_of(t["gate_bias"])))
            with eng.Fori(0, NE // NR - 1) as k:
                for i in range(NR):
                    e_y.wait(eng, k, i + 1)
                    load_expert(k * NR + (NR + i), i)
            e_fin.wait(eng, 0, 1)
            e_out.done(eng.dma_start(out, y_out[:, :]))
            e_out.wait(eng, 0, 1)

        @block.gpsimd
        def _(eng):
            eng.memset(ident[:, :], 0.0).then_inc(e_pool.sem, 1)
            e_pool.wait(eng, 0, 1)
            eng.affine_select(out=ident[:, :], in_=ident[:, :], compare_op=ALU.not_equal, fill=1.0,
                              base=0, pattern=[[-1, P]], channel_multiplier=1).then_inc(e_pool.sem, 1)
            for b in p_sb + o_st + qz_hi + qz_lo:
                n = 1
                for d in b.shape[1:]:
                    n *= d
                v = b[:, :] if len(b.shape) == 2 else b[:, :, :]
                eng.memset(v.bitcast(F32) if b.dtype == F32R else v, 0.0).then_inc(e_pool.sem, 1)
            eng.memset(zero_col, 0.0).then_inc(e_pool.sem, 1)
            eng.memset(nm_init, BIG).then_inc(e_pool.sem, 1)
            for l in l_st:
                eng.memset(l, 0.0).then_inc(e_pool.sem, 1)

            for v, x in ((ln_eps, LN_EPS), (rms_eps, RMS_EPS), (minus_half, -0.5), (one_col, 1.0)):
                eng.memset(v, x).then_inc(e_pool.sem, 1)
            e_pool.wait(eng, 0, N_POOL)

            def rsqrt(dst, src, eps):
                eng.tensor_tensor(r_t, src, eps, ALU.add).then_inc(e_pool.sem, 1)
                n_pool[0] += 1
                e_pool.wait(eng, 0, n_pool[0])
                e_rs.done(eng.tensor_tensor(dst, r_t, minus_half, ALU.pow))

            n_pool = [N_POOL]
            e_var.wait(eng, 0, 1)
            rsqrt(rstd, mv[:, 1:2], ln_eps)
            e_act.wait(eng, 0, 2)
            rsqrt(q_r, q_ss, rms_eps)

            def key_norm(s, j):
                e_sq.wait(eng, s, j + 1)
                e_rt.done(eng.tensor_tensor(k_t[:, j:j + 1], k_ss[:, j:j + 1], rms_eps, ALU.add))
                e_rt.wait(eng, s, j + 1)
                e_r.done(eng.tensor_tensor(k_r[:, j:j + 1], k_t[:, j:j + 1], minus_half, ALU.pow))

            def step(eng, s, par, loop=False):
                proj, _, _ = parts(s, loop)
                if not proj:
                    return
                e_cx.wait(eng, s, 1)
                for j in range(GT):
                    src = cx[par][:, :, j * P:(j + 1) * P]
                    if loop or s > 0 or j >= 2:
                        e_vp.wait(eng, s, j + 1 - 2)
                    e_chi.done(eng.tensor_tensor(cx_hi[j % 2][:, :, :], src, one_col.unsqueeze(2).broadcast_to((P, DC, P)),
                                                 ALU.mult))
                    e_chi.wait(eng, s, j + 1)
                    e_clo.done(eng.tensor_tensor(cx_lo[j % 2][:, :, :], src,
                                                 cx_hi[j % 2][:, :, :].bitcast(F32), ALU.subtract))
                    if j:
                        key_norm(s, j - 1)
                key_norm(s, GT - 1)

            steps(eng, step)
            e_var.wait(eng, 0, 2)
            rsqrt(rstd, mv[:, 1:2], ln_eps)
            e_so.wait(eng, 0, NB)
            eng.memset(earlier[:, :, :], 1.0).then_inc(e_pool.sem, 1)
            n_pool[0] += 1
            e_pool.wait(eng, 0, n_pool[0])
            e_tri.done(eng.affine_select(out=earlier[:, :, :], in_=earlier[:, :, :], compare_op=ALU.is_gt, fill=0.0,
                                         base=0, pattern=[[1, NE], [-1, NE]], channel_multiplier=0))
            e_var.wait(eng, 0, 3)
            rsqrt(rstd, mv[:, 1:2], ln_eps)

        @block.scalar
        def _(eng):
            copy, exp, square = ACT.Copy, ACT.Exp, ACT.Square
            e_pe.wait(eng, 0, 1)
            e_act.done(eng.activation(xnt[:, :], ps_t[:, :], copy))
            e_dve.wait(eng, 0, 3)
            e_act.done(eng.activation(ot_sb[:, :], qf[:, :], square, scale=D ** -0.5, accum_out=q_ss))
            e_pool.wait(eng, 0, N_POOL)
            for i in range(2):
                e_pe.wait(eng, 0, 3 + i)
                for j in range(HC):
                    e_act.done(eng.activation(qz_hi[i][j * HD:(j + 1) * HD, j::HC, :],
                                              ps_t[j * HD:(j + 1) * HD, :].rearrange("p (c q) -> p c q", c=DC), copy))
            for i in range(4):
                e_w[i].wait(eng, 0, 1)
                e_whi.done(eng.activation(w_hi[i][:, :, :], stage[i][:, :, :], copy))
            e_wlo.wait(eng, 0, 4)

            def step(eng, s, par, loop=False):
                proj, score, end = parts(s, loop)
                g = s - 1
                lo, hi = mask(s, loop)
                for h in range(NH):
                    j = h // 4
                    if score:
                        e_nm.wait(eng, g, h + 1)
                        if loop or g > 0 or h >= NP:
                            e_pt.wait(eng, g, h + 1 - NP)
                        pb = p_sb[h % NP]
                        if not loop and s == 2:
                            e_mask.done(eng.activation(pb[:, 0:1], zero_col, copy))
                        e_exp.done(eng.activation(pb[:, lo:hi], ps_s[h % NS][:, lo:hi], exp,
                                                  bias=nm[1 - par][:, h:h + 1], accum_out=ls[1 - par][:, h:h + 1]))
                    if end and h == 3:
                        e_pv.wait(eng, s - 2, NH)
                        if loop or s > 2:
                            e_ot.wait(eng, s - 2, 0)
                        e_oc.done(eng.activation(ot_sb[:, :], ps_o[:, :], copy))
                    if proj and h % 4 == 0:
                        e_kb.wait(eng, s, j + 1)
                        if loop or s > 0 or j >= 2:
                            e_kt.wait(eng, s, j + 1 - 2)
                        e_sq.done(eng.activation(kn[j % 2][:, :], kb[j % 2][:, :], square, scale=D ** -0.5,
                                                 accum_out=k_ss[:, j:j + 1]))
                        e_r.wait(eng, s, j + 1)
                        e_kn.done(eng.activation(kn[j % 2][:, :], kb[j % 2][:, :], copy, scale=k_r[:, j:j + 1]))
                    if proj and h % 4 == 2:
                        e_kt.wait(eng, s, j + 1)
                        e_khi.done(eng.activation(kt_hi[par][:, :, j * P:(j + 1) * P],
                                                  ps_t[:, :].rearrange("p (c k) -> p c k", c=DC), copy))
                    if proj and h % 4 == 3:
                        e_vp.wait(eng, s, j + 1)
                        if loop or s >= 2:
                            e_pv.wait(eng, s - 2, NH)
                        e_v.done(eng.activation(v_sb[par][:, j, :], ps_v[:, :], copy))
                if score:
                    e_dm.wait(eng, g, 1)
                    if loop or g > 0:
                        e_osc.wait(eng, g, 0)
                    e_al.done(eng.activation(al, dm, exp))

            steps(eng, step)
            e_pe.wait(eng, 0, 5)
            e_act.done(eng.activation(xnt[:, :], ps_t[:, :], copy))

            e_lnt.wait(eng, 0, 1)
            e_lntc.done(eng.activation(ynt[:, :], ps_t[:, :], copy))
            for i, dst in enumerate((sqt, skt)):
                for b in range(NB):
                    e_tr.wait(eng, 0, NB * i + b + 1)
                    e_trc.done(eng.activation(dst[:, b * 512:(b + 1) * 512], ps_tr[b % 2][:, :], copy))
            for b in range(NB):
                e_smax.wait(eng, 0, b + 1)
                for i in range(HB):
                    h = b * HB + i
                    e_sexp.done(eng.activation(sp[:, h * P:(h + 1) * P], ps_sc[b][:, i * P:(i + 1) * P], exp,
                                               bias=s_nb[:, h:h + 1], scale=SD ** -0.5, accum_out=s_sum[:, h:h + 1]))
            for b in range(NB):
                e_spt.wait(eng, 0, b + 1)
                e_sptc.done(eng.activation(spt[:, b * 512:(b + 1) * 512], ps_tr[b % 2][:, :], copy))
                if b:
                    e_so.wait(eng, 0, b)
                    e_soc.done(eng.activation(sot[:, (b - 1) * 512:b * 512], ps_sc[b - 1][:, :], copy))
            e_so.wait(eng, 0, NB)
            e_soc.done(eng.activation(sot[:, (NB - 1) * 512:], ps_sc[NB - 1][:, :], copy))

            e_lnt.wait(eng, 0, 2)
            e_lntc.done(eng.activation(x3t[:, :], ps_t[:, :], copy))
            e_lg.wait(eng, 0, 1)
            e_lge.done(eng.activation(score, ps_lg[:, 0:NE], exp, scale=-1.0))
            e_sg.wait(eng, 0, 2)
            e_sge.done(eng.activation(sh_e[:, :], ps_sg[:, :], exp, scale=-1.0))
            e_sht.wait(eng, 0, 1)
            e_shtc.done(eng.activation(sh_ht[:, :], ps_t[:, :], copy))
            with eng.Fori(0, NE // NR) as k:
                for i in range(NR):
                    e_h.wait(eng, k, i + 1)
                    e_he.done(eng.activation(m_e[i % 2][:, :], ps_h[i % 2][:, 0:NF], exp, scale=-1.0))
                    e_ht.wait(eng, k, i + 1)
                    e_htc.done(eng.activation(m_ht[i % 2][:, :], ps_ht[i % 2][:, 0:NF], copy))

        @block.vector
        def _(eng):
            def chain(ins):
                n = e_dve.done(ins)
                e_dve.wait(eng, 0, n)
                return n

            n_rsqrt = iter((1, 3, 4))

            def layernorm(dst, src, done=None):
                chain(eng.bn_stats(stats, src))
                e_var.done(eng.bn_aggr(mv, stats))
                e_rs.wait(eng, 0, next(n_rsqrt))
                last = eng.tensor_scalar(dst, src, mv[:, 0:1], rstd, ALU.subtract, ALU.mult)
                return chain(last) if done is None else done.done(last)

            e_x.wait(eng, 0, 1)
            layernorm(xn[:, :], x_sb[:, :])
            e_rows.wait(eng, 0, 9)
            e_pe.wait(eng, 0, 2)
            chain(eng.tensor_tensor(qf[:, :], ps_k[:, :], q_rows[:, 0, :], ALU.add))
            e_rs.wait(eng, 0, 2)
            chain(eng.scalar_tensor_tensor(qn[:, :], qf[:, :], q_r, q_rows[:, 1, :], ALU.mult, ALU.mult))
            for i in range(2):
                if i:
                    e_pe.wait(eng, 0, 3)
                chain(eng.scalar_tensor_tensor(qf[:, :], qn[:, :], HD ** -0.5, q_rows[:, 2 + i, :], ALU.mult, ALU.mult))
                for j in range(HC):
                    e_act.wait(eng, 0, 2 + HC * (i + 1))
                    r = slice(j * HD, (j + 1) * HD)
                    chain(eng.tensor_tensor(qz_lo[i][r, j::HC, :], ps_t[r, :].rearrange("p (c q) -> p c q", c=DC),
                                            qz_hi[i][r, j::HC, :].bitcast(F32), ALU.subtract))
            for i in range(4):
                e_whi.wait(eng, 0, i + 1)
                e_wlo.done(eng.tensor_tensor(w_lo[i][:, :, :], stage[i][:, :, :], w_hi[i][:, :, :].bitcast(F32),
                                             ALU.subtract))
            e_wlo.wait(eng, 0, 4)
            e_pool.wait(eng, 0, N_POOL)

            def step(eng, s, par, loop=False):
                proj, score, end = parts(s, loop)
                g = s - 1
                lo, hi = mask(s, loop)
                st = 0 if (not loop and s == 2) else 1
                for h in range(NH):
                    j = h // 4
                    if score:
                        old = nm_init if (not loop and s in (1, 2)) else nm[par]
                        e_qk.wait(eng, g, h + 1)
                        e_gm.done(eng.tensor_reduce(ngm[:, h:h + 1], ps_s[h % NS][:, lo:hi], AX.X, ALU.max, negate=True))
                        e_gm.wait(eng, g, h + 1)
                        e_nm.done(eng.tensor_tensor(nm[1 - par][:, h:h + 1], ngm[:, h:h + 1], old[:, h:h + 1], ALU.min))
                    if proj and h % 4 == 0:
                        e_kp.wait(eng, s, j + 1)
                        if loop or s > 0 or j >= 2:
                            e_kn.wait(eng, s, j + 1 - 2)
                        bias = k_bias[:, 0 if (not loop and s == 0) else 1, :]
                        e_kb.done(eng.tensor_tensor(kb[j % 2][:, :], ps_k[:, :], bias, ALU.add))
                    gp, hp = (g, h - 2) if h >= 2 else (g - 1, h - 2 + NH)
                    if (score and h >= 2) or (end and h < 2):
                        e_pt.wait(eng, gp, hp + 1)
                        if loop or s >= 2 or h >= 4:
                            e_pv.wait(eng, gp, hp + 1 - 2)
                        e_pte.done(eng.tensor_copy(pt_sb[hp % 2][:, :], ps_pt[:, :]))
                    if end and h == 1:
                        e_al.wait(eng, s - 2, 1)
                        if loop or s > 2:
                            e_l2.wait(eng, s - 2, 0)
                            e_oadd.wait(eng, s - 2, 0)
                        e_l1.done(eng.tensor_tensor(l_st[st], l_st[st], al, ALU.mult))
                        e_exp.wait(eng, s - 2, NH)
                        e_l1.wait(eng, s - 2, 1)
                        e_l2.done(eng.tensor_tensor(l_st[st], l_st[st], ls[par], ALU.add))
                        o3 = o_st[st][:, :].rearrange("p (h d) -> p h d", h=NH)
                        e_osc.done(eng.tensor_tensor(o3, o3, al.unsqueeze(2).broadcast_to((P, NH, HD)), ALU.mult))
                    if end and h == 5:
                        e_ot.wait(eng, s - 2, 1)
                        e_osc.wait(eng, s - 2, 1)
                        e_oadd.done(eng.tensor_tensor(o_st[st][:, :], ps_t[:, :], o_st[st][:, :], ALU.add))
                    if proj and h % 4 == 2:
                        e_khi.wait(eng, s, j + 1)
                        part = slice(j * P, (j + 1) * P)
                        e_klo.done(eng.tensor_tensor(kt_lo[par][:, :, part], ps_t[:, :].rearrange("p (c k) -> p c k", c=DC),
                                                     kt_hi[par][:, :, part].bitcast(F32), ALU.subtract))
                if score:
                    e_nm.wait(eng, g, NH)
                    old = nm_init if (not loop and s in (1, 2)) else nm[par]
                    if loop or s >= 2:
                        e_al.wait(eng, g, 0)
                    e_dm.done(eng.tensor_tensor(dm, nm[1 - par], old, ALU.subtract))

            steps(eng, step)
            e_oadd.wait(eng, NG - 1, 1)
            e_l2.wait(eng, NG - 1, 1)
            o3 = [o[:, :].rearrange("p (h d) -> p h d", h=NH) for o in o_st]
            for i in range(2):
                chain(eng.reciprocal(rl, l_st[i]))
                chain(eng.tensor_tensor(o3[i], o3[i], rl.unsqueeze(2).broadcast_to((P, NH, HD)), ALU.mult))
                chain(eng.tensor_tensor(o_st[i][:, :], o_st[i][:, :], o_rows[:, 1 + (1 - i), :], ALU.add))
            e_osum.done(eng.tensor_tensor(o_st[0][:, :], o_st[0][:, :], o_st[1][:, :], ALU.add))
            e_pe.wait(eng, 0, 6)
            chain(eng.tensor_tensor(xn[:, :], ps_k[:, :], o_rows[:, 0, :], ALU.add))
            e_x1.done(eng.tensor_tensor(x1[:, :], xn[:, :], x_sb[:, :], ALU.add))
            e_x1.wait(eng, 0, 1)

            layernorm(yn[:, :], x1[:, :], e_ln)
            for i in range(3):
                dst = (sq, sk, sv)[i]
                e_codes[i].wait(eng, 0, 1)
                for c in range(DC):
                    scale = ring_loaded(eng, i * (DC + 1) + c)
                    e_deq.done(eng.tensor_tensor(codes[i][:, c, :], codes[i][:, c, :], scale[:, :], ALU.mult))
                bias = ring_loaded(eng, i * (DC + 1) + DC)
                for b in range(NB):
                    n = slice(b * 512, (b + 1) * 512)
                    e_pj.wait(eng, 0, NB * i + b + 1)
                    e_pjb.done(eng.tensor_tensor(dst[:, n], ps_pj[b % 2][:, :], bias[:, n], ALU.add))
            for b in range(NB):
                bank = ps_sc[b][:, :].rearrange("p (h k) -> p h k", h=HB)
                hs = slice(b * HB, (b + 1) * HB)
                e_ss.wait(eng, 0, b + 1)
                chain(eng.tensor_reduce(s_max[:, hs], bank, AX.X, ALU.max))
                e_smax.done(eng.tensor_scalar(s_nb[:, hs], s_max[:, hs], -SD ** -0.5, None, ALU.mult))
            for b in range(NB):
                hs = slice(b * HB, (b + 1) * HB)
                e_sexp.wait(eng, 0, (b + 1) * HB)
                chain(eng.reciprocal(s_rec[:, hs], s_sum[:, hs]))
                part = sp[:, b * 512:(b + 1) * 512].rearrange("p (h k) -> p h k", h=HB)
                e_sn.done(eng.tensor_tensor(part, part, s_rec[:, hs].unsqueeze(2).broadcast_to((P, HB, P)), ALU.mult))
            e_codes[3].wait(eng, 0, 1)
            for b in range(NB):
                scale = ring_loaded(eng, 3 * (DC + 1) + b)
                part = codes_o[:, b * HB:(b + 1) * HB, :]
                e_deq.done(eng.tensor_tensor(part, part, scale[:, :].rearrange("p (c f) -> p c f", c=HB), ALU.mult))
            e_bo.wait(eng, 0, 1)
            chain(eng.tensor_tensor(x1[:, :], x1[:, :], bo_row[:, :], ALU.add))
            e_sf.wait(eng, 0, 1)
            e_x2.done(eng.tensor_tensor(x2[:, :], ps_pj[0][:, :], x1[:, :], ALU.add))
            e_x2.wait(eng, 0, 1)

            layernorm(x3[:, :], x2[:, :], e_ln)
            e_gate.wait(eng, 0, 2)
            e_tri.wait(eng, 0, 1)
            e_lge.wait(eng, 0, 1)
            chain(eng.tensor_scalar(score, score, 1.0, None, ALU.add))
            chain(eng.reciprocal(score, score))
            chain(eng.tensor_tensor(sc, score, gate_b[:, :], ALU.add))
            for i in range(NGRP):
                chain(eng.max(top8[:, i, :], sc[:, i * GE:(i + 1) * GE]))
            chain(eng.tensor_tensor(gs, top8[:, :, 0], top8[:, :, 1], ALU.add))

            def ranks(dst, v, n):
                other = v.unsqueeze(1).broadcast_to((P, n, n))
                own = v.unsqueeze(2).broadcast_to((P, n, n))
                a, b = cmp_a[:, 0:n, 0:n], cmp_b[:, 0:n, 0:n]
                chain(eng.tensor_tensor(a, other, own, ALU.is_gt))
                chain(eng.tensor_tensor(b, other, own, ALU.is_equal))
                chain(eng.tensor_tensor(b, b, earlier[:, 0:n, 0:n], ALU.mult))
                chain(eng.tensor_tensor(a, a, b, ALU.add))
                chain(eng.tensor_reduce(dst, a, AX.X, ALU.add))

            ranks(grank, gs, NGRP)
            chain(eng.tensor_scalar(gmask, grank, float(TOPG), None, ALU.is_lt))
            chain(eng.tensor_tensor(tmp.rearrange("p (g e) -> p g e", g=NGRP), sc.rearrange("p (g e) -> p g e", g=NGRP),
                                    gmask.unsqueeze(2).broadcast_to((P, NGRP, GE)), ALU.mult))
            ranks(rank, tmp, NE)
            chain(eng.tensor_scalar(sel, rank, float(TOPK), None, ALU.is_lt))
            chain(eng.tensor_tensor(gw, score, sel, ALU.mult))
            chain(eng.tensor_reduce(wsum, gw, AX.X, ALU.add))
            chain(eng.tensor_scalar(wsum, wsum, 1e-20, None, ALU.add))
            chain(eng.reciprocal(wrec, wsum))
            e_gw.done(eng.tensor_scalar(gw, gw, wrec, RSCALE, ALU.mult, ALU.mult))
            e_gw.wait(eng, 0, 1)

            e_sge.wait(eng, 0, 1)
            chain(eng.tensor_scalar(sh_e[:, :], sh_e[:, :], 1.0, None, ALU.add))
            chain(eng.reciprocal(sh_e[:, :], sh_e[:, :]))
            chain(eng.tensor_tensor(sh_a[:, :], ps_sg[:, :], sh_e[:, :], ALU.mult))
            e_shh.done(eng.tensor_tensor(sh_h[:, :], ps_su[:, :], sh_a[:, :], ALU.mult))

            with eng.Fori(0, NE // NR) as k:
                e_gc.done(eng.tensor_copy(g_col[:, :], gw[:, bass.ds(k * NR, NR)]))
                e_gc.wait(eng, k, 1)
                for i in range(NR):
                    m = m_e[i % 2][:, :]
                    e_he.wait(eng, k, i + 1)
                    e_m1.done(eng.tensor_scalar(m, m, 1.0, None, ALU.add))
                    e_m1.wait(eng, k, i + 1)
                    e_m2.done(eng.reciprocal(m, m))
                    e_m2.wait(eng, k, i + 1)
                    e_m3.done(eng.scalar_tensor_tensor(m, ps_h[i % 2][:, 0:NF], g_col[:, i:i + 1], m, ALU.mult, ALU.mult))
                    e_m3.wait(eng, k, i + 1)
                    e_hid.done(eng.tensor_tensor(m_h[i % 2][:, :], ps_h[i % 2][:, NF:2 * NF], m, ALU.mult))
            e_yd.wait(eng, 0, 1)
            e_fin.done(eng.tensor_tensor(y_out[:, :], ps_y[:, :], x2[:, :], ALU.add))

        @block.tensor
        def _(eng):
            def transposes(dst, src):
                for c in range(4):
                    last = eng.transpose(dst[:, c * P:(c + 1) * P], src[:, c * P:(c + 1) * P], ident[:, :])
                return last

            def split_product(dst, a, b):
                n = len(a) * 3
                k = 0
                for (a_hi, a_lo), (b_hi, b_lo) in zip(a, b):
                    for x, y in ((a_hi, b_hi), (a_hi, b_lo), (a_lo, b_hi)):
                        last = eng.matmul(dst, x, y, start=(k == 0), stop=(k == n - 1))
                        k += 1
                return last

            e_pool.wait(eng, 0, 2)
            e_dve.wait(eng, 0, 2)
            e_pe.done(transposes(ps_t, xn))
            e_act.wait(eng, 0, 1)
            e_wq.wait(eng, 0, 1)
            for c in range(DC):
                last = eng.matmul(ps_k[:, :], xnt[:, c * P:(c + 1) * P], wq[:, c, :], start=(c == 0), stop=(c == DC - 1))
            e_pe.done(last)
            for i in range(2):
                e_dve.wait(eng, 0, 5 + 5 * i)
                e_pe.done(transposes(ps_t, qf))
            e_wlo.wait(eng, 0, 2)

            def step(eng, s, par, loop=False):
                proj, score, end = parts(s, loop)
                g = s - 1
                wi = 0 if (not loop and s == 0) else 2
                qi = 0 if (not loop and s == 1) else 1
                if not loop and s == 1:
                    e_dve.wait(eng, 0, 14)
                    e_wlo.wait(eng, 0, 4)
                for h in range(NH):
                    c, j = h // HC, h // 4
                    if score:
                        if h == 0:
                            e_klo.wait(eng, g, GT)
                        if loop or g > 0 or h >= NS:
                            e_exp.wait(eng, g, h + 1 - NS)
                        e_qk.done(split_product(ps_s[h % NS][:, :], [(qz_hi[qi][:, h, :], qz_lo[qi][:, h, :])],
                                                [(kt_hi[1 - par][:, c, :], kt_lo[1 - par][:, c, :])]))
                    if proj and h % 4 in (0, 1):
                        i = h % 4
                        bank, e_read, e_end = ((ps_k, e_kb, e_kp), (ps_v, e_v, e_vp))[i]
                        e_clo.wait(eng, s, j + 1)
                        if loop or s > 0 or j > 0:
                            e_read.wait(eng, s, j)
                        halves = [(cx_hi[j % 2][:, k, :], cx_lo[j % 2][:, k, :]) for k in range(DC)]
                        w = [(w_hi[wi + i][:, k, :], w_lo[wi + i][:, k, :]) for k in range(DC)]
                        e_end.done(split_product(bank[:, :], halves, w))
                    if proj and h % 4 == 2:
                        e_kn.wait(eng, s, j + 1)
                        if j == 1 and end:
                            e_oadd.wait(eng, s - 2, 1)
                        if loop or s > 0 or j > 0:
                            e_klo.wait(eng, s, j)
                        e_kt.done(transposes(ps_t, kn[j % 2]))
                    gp, hp = (g, h - 2) if h >= 2 else (g - 1, h - 2 + NH)
                    if (score and h >= 2) or (end and h < 2):
                        e_exp.wait(eng, gp, hp + 1)
                        if loop or s >= 2 or h > 2:
                            e_pte.wait(eng, gp, hp)
                        e_pt.done(transposes(ps_pt, p_sb[hp % NP]))
                    gp, hp = (g, h - 3) if h >= 3 else (g - 1, h - 3 + NH)
                    if (score and h >= 3) or (end and h < 3):
                        e_pte.wait(eng, gp, hp + 1)
                        if h == 3:
                            e_v.wait(eng, g, GT)
                            if loop or g > 0:
                                e_oc.wait(eng, g, 0)
                        cp, jp = hp // HC, hp % HC
                        vb = v_sb[1 - par] if h >= 3 else v_sb[par]
                        for k in range(GT):
                            last = eng.matmul(ps_o[jp * HD:(jp + 1) * HD, cp * P:(cp + 1) * P],
                                              vb[:, k, hp * HD:(hp + 1) * HD], pt_sb[hp % 2][:, k * P:(k + 1) * P],
                                              start=(k == 0), stop=(k == GT - 1))
                        e_pv.done(last)
                    if end and h == 5:
                        e_oc.wait(eng, s - 2, 1)
                        if proj:
                            e_klo.wait(eng, s, 1)
                        e_ot.done(transposes(ps_t, ot_sb))

            steps(eng, step)
            e_osum.wait(eng, 0, 1)
            e_pe.done(transposes(ps_t, o_st[0]))
            e_act.wait(eng, 0, 11)
            e_wo.wait(eng, 0, 1)
            for c in range(DC):
                last = eng.matmul(ps_k[:, :], xnt[:, c * P:(c + 1) * P], wo[:, c, :], start=(c == 0), stop=(c == DC - 1))
            e_pe.done(last)

            e_ln.wait(eng, 0, 1)
            e_lnt.done(transposes(ps_t, yn))
            e_lntc.wait(eng, 0, 1)
            for i in range(3):
                e_deq.wait(eng, 0, DC * (i + 1))
                for b in range(NB):
                    if NB * i + b >= 2:
                        e_pjb.wait(eng, 0, NB * i + b - 1)
                    for c in range(DC):
                        last = eng.matmul(ps_pj[b % 2][:, :], ynt[:, c * P:(c + 1) * P],
                                          codes[i][:, c, b * 512:(b + 1) * 512], start=(c == 0), stop=(c == DC - 1))
                    e_pj.done(last)
                if i:
                    for b in range(NB):
                        n = NB * (i - 1) + b
                        e_pjb.wait(eng, 0, n + 1)
                        if n >= 2:
                            e_trc.wait(eng, 0, n - 1)
                        e_tr.done(transposes(ps_tr[b % 2], (sq, sk)[i - 1][:, b * 512:(b + 1) * 512]))
            e_trc.wait(eng, 0, 2 * NB)
            for b in range(NB):
                for h in range(b * HB, (b + 1) * HB):
                    part = slice(h * P, (h + 1) * P)
                    last = eng.matmul(ps_sc[b][:, (h % HB) * P:(h % HB + 1) * P], sqt[:, part], skt[:, part], start=True, stop=True)
                e_ss.done(last)
            for b in range(NB + 1):
                if b < NB:
                    e_sn.wait(eng, 0, b + 1)
                    if b >= 2:
                        e_sptc.wait(eng, 0, b - 1)
                    e_spt.done(transposes(ps_tr[b % 2], sp[:, b * 512:(b + 1) * 512]))
                if b:
                    e_sptc.wait(eng, 0, b)
                    for h in range((b - 1) * HB, b * HB):
                        part = slice(h * P, (h + 1) * P)
                        last = eng.matmul(ps_sc[b - 1][:, (h % HB) * P:(h % HB + 1) * P], sv[:, part], spt[:, part], start=True, stop=True)
                    e_so.done(last)
            e_soc.wait(eng, 0, NB)
            e_deq.wait(eng, 0, 3 * DC + NB)
            for h in range(SH):
                last = eng.matmul(ps_pj[0][:, :], sot[:, h * P:(h + 1) * P], codes_o[:, h, :], start=(h == 0), stop=(h == SH - 1))
            e_sf.done(last)

            e_ln.wait(eng, 0, 2)
            e_lnt.done(transposes(ps_t, x3))
            e_lntc.wait(eng, 0, 2)
            e_gate.wait(eng, 0, 2)

            def times_x3(dst, w):
                for c in range(DC):
                    last = eng.matmul(dst, x3t[:, c * P:(c + 1) * P], w[:, c, :], start=(c == 0), stop=(c == DC - 1))
                return last

            e_lg.done(times_x3(ps_lg[:, 0:NE], gate_w))
            e_shw.wait(eng, 0, 3)
            e_sg.done(times_x3(ps_sg[:, :], sh_w[0]))
            e_sg.done(times_x3(ps_su[:, :], sh_w[1]))
            e_shh.wait(eng, 0, 1)
            e_sht.done(transposes(ps_t, sh_h))
            e_shtc.wait(eng, 0, 1)

            def shared_down(c):
                return eng.matmul(ps_y[:, :], sh_ht[:, c * P:(c + 1) * P], sh_w[2][:, c, :], start=(c == 0), stop=(c == DC - 1),
                                  skip_group_check=True)

            def expert_up(k, i):
                e_ew[i % NR].wait(eng, k + i // NR, 1)
                if not isinstance(k, int) or k * NR + i > 1:
                    e_hid.wait(eng, k, i - 1)
                e_h.done(times_x3(ps_h[i % 2][:, :], w13[i % NR]))

            def expert_down(k, i):
                e_hid.wait(eng, k, i + 1)
                for c in range(NF // P):
                    last = eng.transpose(ps_ht[i % 2][:, c * P:(c + 1) * P], m_h[i % 2][:, c * P:(c + 1) * P], ident[:, :])
                e_ht.done(last)
                e_htc.wait(eng, k, i + 1)
                for c in range(NF // P):
                    last = eng.matmul(ps_y[:, :], m_ht[i % 2][:, c * P:(c + 1) * P], w2[i][:, c, :], start=False, stop=False,
                                      skip_group_check=True)
                e_y.done(last)

            def experts(k, final=False):
                for i in range(NR):
                    if not final or i + 1 < NR:
                        expert_up(k, i + 1)
                    expert_down(k, i)

            shared_down(0)
            expert_up(0, 0)
            experts(0)
            with eng.Fori(1, NE // NR - 1) as k:
                experts(k)
            experts(NE // NR - 1, final=True)
            for c in range(1, DC):
                last = shared_down(c)
            e_yd.done(last)


NAMES = ["q_b", "k_b", "v_b", "k_img_b", "v_img_b", "o_b", "norm_q_w", "norm_k_w", "norm_k_img_w"]


def kernel(**inputs):
    import numpy as np
    import concourse.bacc as bacc
    from concourse import mybir as mb
    from concourse.bass_utils import run_bass_kernel_spmd as run

    def lay(a):
        return np.ascontiguousarray(np.asarray(a))

    arrays = {"x": lay(inputs["x"][0]), "ctx_t": lay(np.asarray(inputs["ctx_2048"])[0].T)}
    for n in NAMES:
        arrays[n] = lay(inputs["L0_xattn_" + n])
    for n in ["q", "k", "v", "k_img", "v_img", "o"]:
        arrays[n + "_wt"] = lay(np.asarray(inputs[f"L0_xattn_{n}_w"]).T)
    for n in "qkvo":
        for part in ("codes", "scales"):
            arrays[f"w{n}_{part}"] = lay(inputs[f"L0_attn_w{n}_{part}"])
        arrays["b" + n] = lay(inputs["L0_attn_b" + n])
    for n in ("w1", "w2", "w3", "gate_bias", "shared_gate", "shared_up", "shared_down"):
        arrays[n] = lay(inputs["L0_ffn_" + n])
    arrays["gate_wt"] = lay(np.asarray(inputs["L0_ffn_gate_w"]).T)
    nc = bacc.Bacc("TRN2", target_bir_lowering=False, num_devices=1)
    t = {n: nc.dram_tensor(n, a.shape, mb.dt.from_np(a.dtype), kind="ExternalInput").ap() for n, a in arrays.items()}
    out = nc.dram_tensor("out", (P, D), mb.dt.float32, kind="ExternalOutput").ap()
    program(nc, t, out)
    r = run(nc, [arrays], core_ids=[0])
    return r.results[0]["out"].reshape(1, P, D)
```

```python
import concourse.bass as bass
from concourse import mybir
from contextlib import ExitStack

F32 = mybir.dt.float32
F32R = mybir.dt.float32r
ALU = mybir.AluOpType
ACT = mybir.ActivationFunctionType
AX = mybir.AxisListType

P = 128
D = 512
DC = D // P
NH, HD = 16, 32
HC = P // HD
NK = 12544
IMG = 257
GK = 512
GT = GK // P
TXT0 = IMG - 1
NG = 1 + (NK - TXT0) // GK
assert TXT0 + (NG - 1) * GK == NK and IMG <= GK
SH, SD = 16, 128
SF = SH * SD
HB = 4
NB = SH // HB
QB = 32
NE, NF = 32, 256
NGRP, TOPG, TOPK = 4, 2, 4
GE = NE // NGRP
FS = 512
RSCALE = 2.0
BIG = 3.0e38
LN_EPS, RMS_EPS = 1e-5, 1e-6


class Event:

    def __init__(self, sem, per=0, by=1):
        self.sem, self.per, self.by, self.n = sem, per, by, 0

    def done(self, ins):
        ins.then_inc(self.sem, self.by)
        self.n += 1
        return self.n

    def part(self, ins):
        ins.then_inc(self.sem, 16)

    def wait(self, eng, rnd, n):
        eng.wait_ge(self.sem, (rnd * self.per + n) * self.by)


def program(nc, t, out):
    ctx = ExitStack()
    with ctx:
        base = (nc.sbuf_base + 31) // 32 * 32
        KB = 1024
        ctx.enter_context(nc.sbuf_tensor("arena", [P, 207 * KB // 4 + 128], F32))

        def sb(name, off, shape, dt=F32):
            return nc.alloc_sbuf_tensor_at(name, shape, dt, offset=base + off)

        def event(name, per=0, by=1):
            return Event(ctx.enter_context(nc.semaphore(name)), per, by)

        W_NAMES = ["k_img", "v_img", "k", "v"]
        RAW_AT, W_AT = (0, 8, 32, 40), (64, 80, 0, 16)
        w_hi = [sb(f"w_hi_{n}", W_AT[i] * KB, [P, DC, D], F32R) for i, n in enumerate(W_NAMES)]
        w_lo = [sb(f"w_lo_{n}", (W_AT[i] + 8) * KB, [P, DC, D], F32R) for i, n in enumerate(W_NAMES)]
        stage = [sb(f"stage_{n}", RAW_AT[i] * KB, [P, DC, D]) for i, n in enumerate(W_NAMES)]
        wq = sb("wq", 16 * KB, [P, DC, D])
        q_rows = sb("q_rows", 24 * KB, [P, 4, D])
        NST = 3
        stk = [sb(f"k_stack{i}", (32 + 32 * i) * KB, [P, NH, GK], F32R) for i in range(2)]
        q_st = [sb(f"q_stack{i}", (96 + 8 * i) * KB, [P, NH, P], F32R) for i in range(2)]
        kt_hi, kt_lo = sb("kt_hi", 112 * KB, [P, DC, GK], F32R), sb("kt_lo", 120 * KB, [P, DC, GK], F32R)
        v_sb = [sb(f"v_sb{i}", (128 + 8 * i) * KB, [P, GT, D]) for i in range(2)]
        cx = sb("cx", 144 * KB, [P, DC, GK])
        cx_hi, cx_lo = sb("cx_hi", 152 * KB, [P, DC, GK], F32R), sb("cx_lo", 160 * KB, [P, DC, GK], F32R)
        kb = [sb(f"kb{i}", (168 + 2 * i) * KB, [P, D]) for i in range(2)]
        kn = [sb(f"kn{i}", (172 + 2 * i) * KB, [P, D]) for i in range(2)]
        NP = 4
        p_sb = [sb(f"p{i}", (176 + 2 * i) * KB, [P, GK]) for i in range(NP)]
        pt_sb = [sb(f"pt{i}", (184 + 2 * i) * KB, [P, GK]) for i in range(2)]
        k_bias = sb("k_bias", 188 * KB, [P, 2, D])
        ot_sb = sb("ot_sb", 192 * KB, [P, D])
        o_st = [sb(f"o_st{i}", (194 + 2 * i) * KB, [P, D]) for i in range(2)]
        x_sb = sb("x_sb", 198 * KB, [P, D])
        o_rows = sb("o_rows", 200 * KB, [P, 3, D])
        ident = sb("ident", 206 * KB, [P, P])
        small = sb("small", 206 * KB + 512, [P, 256])
        cols = iter(range(0, 256, 16))
        nm = [small[:, c:c + NH] for c in (next(cols), next(cols))]
        nm_init, ngm, dm, al = (small[:, c:c + NH] for c in (next(cols), next(cols), next(cols), next(cols)))
        ls = [small[:, c:c + NH] for c in (next(cols), next(cols))]
        l_st = [small[:, c:c + NH] for c in (next(cols), next(cols))]
        c = next(cols)
        k_ss, k_r = small[:, c:c + GT], small[:, c + GT:c + 2 * GT]
        c = next(cols)
        stats, mv, rstd, q_ss, q_r = (small[:, c:c + 6], small[:, c + 6:c + 8], small[:, c + 8:c + 9],
                                      small[:, c + 9:c + 10], small[:, c + 10:c + 11])
        rl = small[:, 192:192 + NH]
        zero_col, ln_eps, rms_eps, minus_half = (small[:, i:i + 1] for i in range(208, 212))
        one_col = small[:, 221:222]
        k_t, r_t = small[:, 212:212 + GT], small[:, 220:221]
        wo = sb("wo", 96 * KB, [P, DC, D])
        xn, xnt, qf, qn = kb[0], kb[1], kn[0], kn[1]

        codes = [sb(f"codes_{n}", 32 * i * KB, [P, DC, SF]) for i, n in enumerate("qkv")]
        codes_o = sb("codes_o", 96 * KB, [P, SH, D])
        NRING = 3
        ring = [sb(f"scale_ring{i}", (128 + 8 * i) * KB, [P, SF]) for i in range(NRING)]
        sv = sb("sv", 152 * KB, [P, SF])
        sq = sb("sq", 160 * KB, [P, SF])
        sqt = sb("sqt", 168 * KB, [P, SF])
        sk = sb("sk", 176 * KB, [P, SF])
        skt = sb("skt", 184 * KB, [P, SF])
        sp, spt, sot = sq, sk, skt
        bo_row = sb("bo_row", 192 * KB, [P, D])
        x1 = sb("x1", 194 * KB, [P, D])
        yn, ynt = sb("yn", 198 * KB, [P, D]), sb("ynt", 200 * KB, [P, D])
        s_max, s_nb, s_sum, s_rec = (small[:, i:i + SH] for i in (0, 16, 32, 48))

        NR = 8
        w13 = [sb(f"w13_{i}", 12 * i * KB, [P, DC, 2 * NF]) for i in range(NR)]
        w2 = [sb(f"w2_{i}", (12 * i + 8) * KB, [P, NF // P, D]) for i in range(NR)]
        sh_w = [sb(f"shared_{n}", (128 + 8 * i) * KB, [P, DC, FS]) for i, n in enumerate(["gate", "up", "down"])]
        earlier = sb("earlier", 152 * KB, [P, NE, NE])
        gate_w = sb("gate_w", 156 * KB, [P, DC, NE])
        gate_b = sb("gate_b", 156 * KB + 512, [P, NE])
        cmp_a = sb("cmp_a", 160 * KB, [P, NE, NE])
        cmp_b = sb("cmp_b", 164 * KB, [P, NE, NE])
        rt = sb("router", 168 * KB, [P, 16, NE])
        sh_e, sh_a = sb("sh_e", 170 * KB, [P, FS]), sb("sh_a", 172 * KB, [P, FS])
        sh_h, sh_ht = sb("sh_h", 174 * KB, [P, FS]), sb("sh_ht", 176 * KB, [P, FS])
        m_e = [sb(f"m_e{i}", (178 + i) * KB, [P, NF]) for i in range(2)]
        m_h = [sb(f"m_h{i}", (180 + i) * KB, [P, NF]) for i in range(2)]
        m_ht = [sb(f"m_ht{i}", (182 + i) * KB, [P, NF]) for i in range(2)]
        g_col = sb("g_col", 184 * KB, [P, NR])
        x2 = sb("x2", 186 * KB, [P, D])
        x3, x3t = sb("x3", 188 * KB, [P, D]), sb("x3t", 190 * KB, [P, D])
        y_out = sb("y_out", 202 * KB, [P, D])
        score, sc, tmp, sel, gw, rank = (rt[:, i, :] for i in range(6))
        top8 = rt[:, 8, :].rearrange("p (g e) -> p g e", g=NGRP)
        gs, gmask, grank = (rt[:, 9 + i, 0:NGRP] for i in range(3))
        wsum, wrec = rt[:, 14, 0:1], rt[:, 15, 0:1]

        ps = [ctx.enter_context(nc.psum_tensor(f"ps{i}", [P, 512], F32)) for i in range(8)]
        ps_a, ps_t, ps_pt, ps_o = ps[0:2], ps[2], (ps[3], ps[7]), ps[4]
        ps_s = ps[5:7]
        NS = len(ps_s)

        e_x = event("x_loaded", by=16)
        e_wq = event("wq_loaded", by=16)
        e_rows = event("rows_loaded", by=16)
        e_w = [event(f"w_loaded_{n}", by=16) for n in W_NAMES]
        e_pool = event("pool_init")
        e_dve, e_act, e_pe = event("dve_chain"), event("act_chain"), event("pe_chain")
        e_whi, e_wlo = event("w_hi_split"), event("w_lo_split")
        e_cx = event("cx_loaded", 1, 16)
        e_chi, e_clo = event("cx_hi", GT), event("cx_lo", GT)
        e_kp, e_vp = event("k_projected", GT), event("v_projected", GT)
        e_kb, e_sq, e_r, e_kn = event("k_biased", GT), event("k_squared", GT), event("k_rms", GT), event("k_normed", GT)
        e_kt, e_khi, e_klo, e_v = event("k_transposed", GT), event("kt_hi", GT), event("kt_lo", GT), event("v_stored", GT)
        HALVES = 2
        e_stk = event("keys_stacked", 1, 16 * HALVES * NST * HC)
        e_qk = event("scores", NH)
        e_gm, e_nm, e_exp = event("group_max", NH), event("running_max", NH), event("exp", NH)
        e_pt, e_pte, e_pv = event("p_transposed", NH), event("pt_stored", NH), event("pv", NH)
        e_dm, e_al, e_l1, e_l2 = event("max_step", 1), event("alpha", 1), event("l_scaled", 1), event("l_added", 1)
        e_osc, e_oc, e_ot, e_oadd = event("o_scaled", 1), event("ot_stored", 1), event("o_transposed", 1), event("o_added", 1)
        e_mask = event("masked", 1)
        e_wo = event("wo_loaded", by=16)
        e_osum, e_x1 = event("attention_summed"), event("x_after_cross")
        e_var, e_rs, e_rt = event("variance"), event("rsqrt"), event("k_mean_square", GT)
        e_out = event("out_stored", by=16)
        e_codes = [event(f"codes_loaded_{n}", by=16) for n in "qkvo"]
        e_ring = [event(f"ring_loaded{i}", by=16 * P // QB) for i in range(NRING)]
        e_bo, e_deq = event("bo_loaded", by=16), event("dequantised")
        e_ln, e_lnt, e_lntc = event("normed"), event("normed_t"), event("normed_t_stored")
        e_pj, e_pjb = event("self_projected"), event("self_biased")
        e_tr, e_trc = event("self_transposed"), event("self_transposed_stored")
        e_ss, e_smax, e_sexp, e_sn = event("self_scores"), event("self_max"), event("self_exp"), event("self_normed")
        e_spt, e_sptc = event("self_p_transposed"), event("self_p_stored")
        e_so, e_soc = event("self_out"), event("self_out_stored")
        e_sf, e_x2 = event("self_final"), event("x_after_self")
        e_shw, e_gate = event("shared_loaded", by=16), event("gate_loaded", by=16)
        e_ew = [event(f"expert_loaded{i}", 1, 48) for i in range(NR)]
        e_lg, e_lge, e_gw = event("logits"), event("logits_exp"), event("gate_weights")
        e_tri = event("earlier_made")
        e_sg, e_sge, e_shh, e_sht, e_shtc = (event(n) for n in ("shared_h", "shared_exp", "shared_hidden",
                                                               "shared_t", "shared_t_stored"))
        e_h, e_he, e_hid, e_ht, e_htc, e_y = (event(n, NR) for n in ("expert_h", "expert_exp", "expert_hidden",
                                                                    "expert_t", "expert_t_stored", "expert_y"))
        e_gc = event("gate_columns", 1)
        e_m1, e_m2, e_m3 = (event(n, NR) for n in ("expert_exp_plus1", "expert_sigmoid", "expert_gate"))
        e_yd, e_fin = event("y_done"), event("finished")

        ps_pj, ps_tr, ps_sc = ps[0:2], ps[2:4], ps[4:8]
        ps_lg, ps_sg, ps_su, ps_y, ps_h, ps_ht = ps[0], ps[1], ps[3], ps[4], ps[5:7], (ps[7], ps[2])

        def rows_of(ap):
            return ap.partition_broadcast(P)

        cxt = t["ctx_t"].rearrange("(c p) k -> p c k", p=P)

        def wview(ap):
            return ap.rearrange("(c p) o -> p c o", p=P)

        def steps(eng, step, peeled=0):
            step(eng, 0, 0)
            step(eng, 1, 1)
            step(eng, 2, 0)
            rounds = (NG - 3) // 2 - peeled
            with eng.Fori(0, rounds) as i:
                step(eng, i * 2 + 3, 1, loop=True)
                step(eng, i * 2 + 4, 0, loop=True)
            for s in range(3 + 2 * rounds, NG + 2):
                step(eng, s, s % 2)

        def parts(s, loop):
            return (loop or s < NG), (loop or 1 <= s <= NG), (loop or s >= 2)

        def mask(s, loop):
            if not loop and s == 1:
                return 0, IMG
            if not loop and s == 2:
                return 1, GK
            return 0, GK

        N_POOL = 2 + NP + 2 + 1 + 1 + 2 + 4
        block = ctx.enter_context(nc.Block())

        def ring_free(eng, item):
            old = item - NRING
            if old < 0:
                return
            i, c = divmod(old, DC + 1)
            if i < 3 and c == DC:
                e_pjb.wait(eng, 0, NB * (i + 1))
            elif i < 3:
                e_deq.wait(eng, 0, i * DC + c + 1)
            else:
                e_deq.wait(eng, 0, 3 * DC + old - 3 * (DC + 1) + 1)

        def ring_loaded(eng, item):
            e_ring[item % NRING].wait(eng, 0, item // NRING + 1)
            return ring[item % NRING]

        @block.sync
        def _(eng):
            e_x.done(eng.dma_start(x_sb[:, :], t["x"]))
            for i in range(2):
                e_w[i].done(eng.dma_start(stage[i][:, :, :], wview(t[W_NAMES[i] + "_wt"])))
            e_wq.done(eng.dma_start(wq[:, :, :], wview(t["q_wt"])))

            def load(g):
                if isinstance(g, int) and g == 0:
                    src = cxt[:, :, 0:GK]
                elif isinstance(g, int):
                    src = cxt[:, :, TXT0 + (g - 1) * GK:TXT0 + g * GK]
                else:
                    src = cxt[:, :, bass.ds(g * GK + (TXT0 - GK), GK)]
                e_cx.done(eng.dma_start(cx[:, :, :], src))

            load(0)
            for i, n in enumerate(["q_b", "norm_q_w", "norm_k_img_w", "norm_k_w"]):
                e_rows.done(eng.dma_start(q_rows[:, i, :], rows_of(t[n])))
            for i, n in enumerate(["k_img_b", "k_b"]):
                e_rows.done(eng.dma_start(k_bias[:, i, :], rows_of(t[n])))
            for i in range(2, 4):
                e_w[i].done(eng.dma_start(stage[i][:, :, :], wview(t[W_NAMES[i] + "_wt"])))
            for i, n in enumerate(["o_b", "v_b", "v_img_b"]):
                e_rows.done(eng.dma_start(o_rows[:, i, :], rows_of(t[n])))

            def step(eng, s, par, loop=False):
                if not loop and s >= NG:
                    return
                if loop or s < NG - 1:
                    e_clo.wait(eng, s, GT)
                    load(s + 1)
                if not loop and s == 0:
                    e_wlo.wait(eng, 0, 4)
                if not loop and s == 1:
                    e_vp.wait(eng, 0, GT)
                for half in range(HALVES):
                    e_klo.wait(eng, s, (half + 1) * GT // HALVES)
                    if half == 0 and (loop or s >= 2):
                        e_qk.wait(eng, s - 2, NH)
                    keys = slice(half * GK // HALVES, (half + 1) * GK // HALVES)
                    for r, part in enumerate((kt_hi, kt_lo, kt_hi)):
                        for j in range(HC):
                            e_stk.part(eng.dma_start(stk[par][r * HD:(r + 1) * HD, j::HC, keys].bitcast(F32),
                                                     part[j * HD:(j + 1) * HD, :, keys].bitcast(F32)))
                if not loop and s == 1:
                    e_qk.wait(eng, 0, NH)
                    e_wo.done(eng.dma_start(wo[:, :, :], wview(t["o_wt"])))

            steps(eng, step, peeled=1)
            e_x1.wait(eng, 0, 1)
            blocks = range(P // QB)
            for i, n in enumerate("qkv"):
                e_codes[i].done(eng.dma_start(codes[i][:, :, :], t[f"w{n}_codes"].rearrange("(c p) f -> p c f", p=P)))
                for c in range(DC):
                    item = i * (DC + 1) + c
                    ring_free(eng, item)
                    for b in blocks:
                        e_ring[item % NRING].part(eng.dma_start(
                            ring[item % NRING][b * QB:(b + 1) * QB, :],
                            t[f"w{n}_scales"][c * len(blocks) + b, :].partition_broadcast(QB)))
                item += 1
                ring_free(eng, item)
                for b in blocks:
                    e_ring[item % NRING].part(eng.dma_start(ring[item % NRING][b * QB:(b + 1) * QB, :],
                                                            t[f"b{n}"].partition_broadcast(QB)))
            e_codes[3].done(eng.dma_start(codes_o[:, :, :], t["wo_codes"].rearrange("(c p) f -> p c f", p=P)))
            so = t["wo_scales"].rearrange("(c b) f -> b c f", b=len(blocks))
            for k in range(NB):
                item = 3 * (DC + 1) + k
                ring_free(eng, item)
                for b in blocks:
                    e_ring[item % NRING].part(eng.dma_start(
                        ring[item % NRING][b * QB:(b + 1) * QB, :].rearrange("p (c f) -> p c f", c=HB),
                        so[b, k * HB:(k + 1) * HB, :].partition_broadcast(QB)))
            e_bo.done(eng.dma_start(bo_row[:, :], rows_of(t["bo"])))

            def load_expert(e, i):
                one = slice(e, e + 1) if isinstance(e, int) else bass.ds(e, 1)
                for half, n in enumerate(("w1", "w3")):
                    e_ew[i].part(eng.dma_start(w13[i][:, :, half * NF:(half + 1) * NF],
                                               t[n][one, :, :].rearrange("o (c p) f -> p (o c) f", p=P)))
                e_ew[i].part(eng.dma_start(w2[i][:, :, :], t["w2"][one, :, :].rearrange("o (c p) f -> p (o c) f", p=P)))

            for i in range(NR):
                last = ((i + 1) * 12 - 1) // 32
                e_pj.wait(eng, 0, NB * (last + 1))
                load_expert(i, i)
            e_deq.wait(eng, 0, 3 * DC + NB)
            for i, n in enumerate(("gate", "up", "down")):
                e_shw.done(eng.dma_start(sh_w[i][:, :, :], t[f"shared_{n}"].rearrange("(c p) f -> p c f", p=P)))
            e_so.wait(eng, 0, NB)
            e_gate.done(eng.dma_start(gate_w[:, :, :], t["gate_wt"].rearrange("(c p) f -> p c f", p=P)))
            e_gate.done(eng.dma_start(gate_b[:, :], rows_of(t["gate_bias"])))
            with eng.Fori(0, NE // NR - 1) as k:
                for i in range(NR):
                    e_y.wait(eng, k, i + 1)
                    load_expert(k * NR + (NR + i), i)
            e_fin.wait(eng, 0, 1)
            e_out.done(eng.dma_start(out, y_out[:, :]))
            e_out.wait(eng, 0, 1)

        @block.gpsimd
        def _(eng):
            eng.memset(ident[:, :], 0.0).then_inc(e_pool.sem, 1)
            e_pool.wait(eng, 0, 1)
            eng.affine_select(out=ident[:, :], in_=ident[:, :], compare_op=ALU.not_equal, fill=1.0,
                              base=0, pattern=[[-1, P]], channel_multiplier=1).then_inc(e_pool.sem, 1)
            for b in p_sb + o_st:
                eng.memset(b[:, :], 0.0).then_inc(e_pool.sem, 1)
            eng.memset(zero_col, 0.0).then_inc(e_pool.sem, 1)
            eng.memset(nm_init, BIG).then_inc(e_pool.sem, 1)
            for l in l_st:
                eng.memset(l, 0.0).then_inc(e_pool.sem, 1)

            for v, x in ((ln_eps, LN_EPS), (rms_eps, RMS_EPS), (minus_half, -0.5), (one_col, 1.0)):
                eng.memset(v, x).then_inc(e_pool.sem, 1)
            e_pool.wait(eng, 0, N_POOL)

            def rsqrt(dst, src, eps):
                eng.tensor_tensor(r_t, src, eps, ALU.add).then_inc(e_pool.sem, 1)
                n_pool[0] += 1
                e_pool.wait(eng, 0, n_pool[0])
                e_rs.done(eng.tensor_tensor(dst, r_t, minus_half, ALU.pow))

            n_pool = [N_POOL]
            e_var.wait(eng, 0, 1)
            rsqrt(rstd, mv[:, 1:2], ln_eps)
            e_act.wait(eng, 0, 2)
            rsqrt(q_r, q_ss, rms_eps)

            def key_norm(s, j):
                e_sq.wait(eng, s, j + 1)
                e_rt.done(eng.tensor_tensor(k_t[:, j:j + 1], k_ss[:, j:j + 1], rms_eps, ALU.add))
                e_rt.wait(eng, s, j + 1)
                e_r.done(eng.tensor_tensor(k_r[:, j:j + 1], k_t[:, j:j + 1], minus_half, ALU.pow))

            def step(eng, s, par, loop=False):
                proj, _, _ = parts(s, loop)
                if not proj:
                    return
                e_cx.wait(eng, s, 1)
                for j in range(GT):
                    part = slice(j * P, (j + 1) * P)
                    if loop or s > 0:
                        e_vp.wait(eng, s, j + 1 - GT)
                    e_chi.done(eng.tensor_tensor(cx_hi[:, :, part], cx[:, :, part],
                                                 one_col.unsqueeze(2).broadcast_to((P, DC, P)), ALU.mult))
                    e_chi.wait(eng, s, j + 1)
                    e_clo.done(eng.tensor_tensor(cx_lo[:, :, part], cx[:, :, part], cx_hi[:, :, part].bitcast(F32),
                                                 ALU.subtract))
                for j in range(GT):
                    key_norm(s, j)

            steps(eng, step)
            e_var.wait(eng, 0, 2)
            rsqrt(rstd, mv[:, 1:2], ln_eps)
            e_so.wait(eng, 0, NB)
            eng.memset(earlier[:, :, :], 1.0).then_inc(e_pool.sem, 1)
            n_pool[0] += 1
            e_pool.wait(eng, 0, n_pool[0])
            e_tri.done(eng.affine_select(out=earlier[:, :, :], in_=earlier[:, :, :], compare_op=ALU.is_gt, fill=0.0,
                                         base=0, pattern=[[1, NE], [-1, NE]], channel_multiplier=0))
            e_var.wait(eng, 0, 3)
            rsqrt(rstd, mv[:, 1:2], ln_eps)

        @block.scalar
        def _(eng):
            copy, exp, square = ACT.Copy, ACT.Exp, ACT.Square
            def split_weight(i):
                e_w[i].wait(eng, 0, 1)
                e_whi.done(eng.activation(w_hi[i][:, :, :], stage[i][:, :, :], copy))

            e_pe.wait(eng, 0, 1)
            e_act.done(eng.activation(xnt[:, :], ps_t[:, :], copy))
            split_weight(0)
            split_weight(1)
            e_dve.wait(eng, 0, 3)
            e_act.done(eng.activation(ot_sb[:, :], qf[:, :], square, scale=D ** -0.5, accum_out=q_ss))
            e_pool.wait(eng, 0, N_POOL)
            for i in range(2):
                e_pe.wait(eng, 0, 3 + i)
                for j in range(HC):
                    head = ps_t[j * HD:(j + 1) * HD, :].rearrange("p (c q) -> p c q", c=DC)
                    for r in range(2):
                        e_act.done(eng.activation(q_st[i][r * HD:(r + 1) * HD, j::HC, :], head, copy))
            e_wlo.wait(eng, 0, 2)
            split_weight(2)
            split_weight(3)

            def step(eng, s, par, loop=False):
                proj, score, end = parts(s, loop)
                g = s - 1
                lo, hi = mask(s, loop)
                for h in range(NH):
                    j = h // 2 - 1
                    if proj and h % 2 == 0 and 0 <= j < GT:
                        e_kb.wait(eng, s, j + 1)
                        if loop or s > 0 or j >= 2:
                            e_kt.wait(eng, s, j + 1 - 2)
                        e_sq.done(eng.activation(kn[j % 2][:, :], kb[j % 2][:, :], square, scale=D ** -0.5,
                                                 accum_out=k_ss[:, j:j + 1]))
                    if score:
                        e_nm.wait(eng, g, h + 1)
                        if loop or g > 0 or h >= NP:
                            e_pt.wait(eng, g, h + 1 - NP)
                        pb = p_sb[h % NP]
                        if not loop and s == 2:
                            e_mask.done(eng.activation(pb[:, 0:1], zero_col, copy))
                        e_exp.done(eng.activation(pb[:, lo:hi], ps_s[h % NS][:, lo:hi], exp,
                                                  bias=nm[1 - par][:, h:h + 1], accum_out=ls[1 - par][:, h:h + 1]))
                    if end and h == 3:
                        e_pv.wait(eng, s - 2, NH)
                        if loop or s > 2:
                            e_ot.wait(eng, s - 2, 0)
                        e_oc.done(eng.activation(ot_sb[:, :], ps_o[:, :], copy))
                    if proj and h % 2 == 0 and 0 <= j < GT:
                        e_r.wait(eng, s, j + 1)
                        e_kn.done(eng.activation(kn[j % 2][:, :], kb[j % 2][:, :], copy, scale=k_r[:, j:j + 1]))
                    j = h // 2 - 2
                    if proj and h % 2 == 0 and 0 <= j < GT:
                        e_kt.wait(eng, s, j + 1)
                        e_khi.done(eng.activation(kt_hi[:, :, j * P:(j + 1) * P],
                                                  ps_t[:, :].rearrange("p (c k) -> p c k", c=DC), copy))
                    j = h // 2 - GT
                    if proj and h % 2 == 1 and j >= 0:
                        e_vp.wait(eng, s, j + 1)
                        if loop or s >= 2:
                            e_pv.wait(eng, s - 2, NH)
                        e_v.done(eng.activation(v_sb[par][:, j, :], ps_a[j % 2][:, :], copy))
                if score:
                    e_dm.wait(eng, g, 1)
                    if loop or g > 0:
                        e_osc.wait(eng, g, 0)
                    e_al.done(eng.activation(al, dm, exp))

            steps(eng, step)
            e_pe.wait(eng, 0, 5)
            e_act.done(eng.activation(xnt[:, :], ps_t[:, :], copy))

            e_lnt.wait(eng, 0, 1)
            e_lntc.done(eng.activation(ynt[:, :], ps_t[:, :], copy))
            for i, dst in enumerate((sqt, skt)):
                for b in range(NB):
                    e_tr.wait(eng, 0, NB * i + b + 1)
                    e_trc.done(eng.activation(dst[:, b * 512:(b + 1) * 512], ps_tr[b % 2][:, :], copy))
            for b in range(NB):
                e_smax.wait(eng, 0, b + 1)
                for i in range(HB):
                    h = b * HB + i
                    e_sexp.done(eng.activation(sp[:, h * P:(h + 1) * P], ps_sc[b][:, i * P:(i + 1) * P], exp,
                                               bias=s_nb[:, h:h + 1], scale=SD ** -0.5, accum_out=s_sum[:, h:h + 1]))
            for b in range(NB):
                e_spt.wait(eng, 0, b + 1)
                e_sptc.done(eng.activation(spt[:, b * 512:(b + 1) * 512], ps_tr[b % 2][:, :], copy))
                if b:
                    e_so.wait(eng, 0, b)
                    e_soc.done(eng.activation(sot[:, (b - 1) * 512:b * 512], ps_sc[b - 1][:, :], copy))
            e_so.wait(eng, 0, NB)
            e_soc.done(eng.activation(sot[:, (NB - 1) * 512:], ps_sc[NB - 1][:, :], copy))

            e_lnt.wait(eng, 0, 2)
            e_lntc.done(eng.activation(x3t[:, :], ps_t[:, :], copy))
            e_lg.wait(eng, 0, 1)
            e_lge.done(eng.activation(score, ps_lg[:, 0:NE], exp, scale=-1.0))
            e_sg.wait(eng, 0, 2)
            e_sge.done(eng.activation(sh_e[:, :], ps_sg[:, :], exp, scale=-1.0))
            e_sht.wait(eng, 0, 1)
            e_shtc.done(eng.activation(sh_ht[:, :], ps_t[:, :], copy))
            with eng.Fori(0, NE // NR) as k:
                for i in range(NR):
                    e_h.wait(eng, k, i + 1)
                    e_he.done(eng.activation(m_e[i % 2][:, :], ps_h[i % 2][:, 0:NF], exp, scale=-1.0))
                    e_ht.wait(eng, k, i + 1)
                    e_htc.done(eng.activation(m_ht[i % 2][:, :], ps_ht[i % 2][:, 0:NF], copy))

        @block.vector
        def _(eng):
            def chain(ins):
                n = e_dve.done(ins)
                e_dve.wait(eng, 0, n)
                return n

            n_rsqrt = iter((1, 3, 4))

            def layernorm(dst, src, done=None):
                chain(eng.bn_stats(stats, src))
                e_var.done(eng.bn_aggr(mv, stats))
                e_rs.wait(eng, 0, next(n_rsqrt))
                last = eng.tensor_scalar(dst, src, mv[:, 0:1], rstd, ALU.subtract, ALU.mult)
                return chain(last) if done is None else done.done(last)

            def split_weight(i):
                e_whi.wait(eng, 0, i + 1)
                e_wlo.done(eng.tensor_tensor(w_lo[i][:, :, :], stage[i][:, :, :], w_hi[i][:, :, :].bitcast(F32),
                                             ALU.subtract))

            e_x.wait(eng, 0, 1)
            layernorm(xn[:, :], x_sb[:, :])
            split_weight(0)
            split_weight(1)
            e_rows.wait(eng, 0, 9)
            e_pe.wait(eng, 0, 2)
            chain(eng.tensor_tensor(qf[:, :], ps_a[0][:, :], q_rows[:, 0, :], ALU.add))
            e_rs.wait(eng, 0, 2)
            chain(eng.scalar_tensor_tensor(qn[:, :], qf[:, :], q_r, q_rows[:, 1, :], ALU.mult, ALU.mult))
            for i in range(2):
                if i:
                    e_pe.wait(eng, 0, 3)
                chain(eng.scalar_tensor_tensor(qf[:, :], qn[:, :], HD ** -0.5, q_rows[:, 2 + i, :], ALU.mult, ALU.mult))
                for j in range(HC):
                    e_act.wait(eng, 0, 2 + 2 * HC * (i + 1))
                    chain(eng.tensor_tensor(q_st[i][2 * HD:3 * HD, j::HC, :],
                                            ps_t[j * HD:(j + 1) * HD, :].rearrange("p (c q) -> p c q", c=DC),
                                            q_st[i][0:HD, j::HC, :].bitcast(F32), ALU.subtract))
            for i in range(2, 4):
                split_weight(i)
            e_wlo.wait(eng, 0, 4)
            e_pool.wait(eng, 0, N_POOL)

            def step(eng, s, par, loop=False):
                proj, score, end = parts(s, loop)
                g = s - 1
                lo, hi = mask(s, loop)
                st = 0 if (not loop and s == 2) else 1
                for h in range(NH):
                    if score:
                        old = nm_init if (not loop and s in (1, 2)) else nm[par]
                        e_qk.wait(eng, g, h + 1)
                        e_gm.done(eng.tensor_reduce(ngm[:, h:h + 1], ps_s[h % NS][:, lo:hi], AX.X, ALU.max, negate=True))
                        e_gm.wait(eng, g, h + 1)
                        e_nm.done(eng.tensor_tensor(nm[1 - par][:, h:h + 1], ngm[:, h:h + 1], old[:, h:h + 1], ALU.min))
                    j = h // 2
                    if proj and h % 2 == 1 and j < GT:
                        e_kp.wait(eng, s, j + 1)
                        if loop or s > 0 or j >= 2:
                            e_kn.wait(eng, s, j + 1 - 2)
                        bias = k_bias[:, 0 if (not loop and s == 0) else 1, :]
                        e_kb.done(eng.tensor_tensor(kb[j % 2][:, :], ps_a[j % 2][:, :], bias, ALU.add))
                    gp, hp = (g, h - 2) if h >= 2 else (g - 1, h - 2 + NH)
                    if (score and h >= 2) or (end and h < 2):
                        e_pt.wait(eng, gp, hp + 1)
                        if loop or s >= 2 or h >= 4:
                            e_pv.wait(eng, gp, hp + 1 - 2)
                        e_pte.done(eng.tensor_copy(pt_sb[hp % 2][:, :], ps_pt[hp % 2][:, :]))
                    if end and h == 1:
                        e_al.wait(eng, s - 2, 1)
                        if loop or s > 2:
                            e_l2.wait(eng, s - 2, 0)
                            e_oadd.wait(eng, s - 2, 0)
                        e_l1.done(eng.tensor_tensor(l_st[st], l_st[st], al, ALU.mult))
                        e_exp.wait(eng, s - 2, NH)
                        e_l1.wait(eng, s - 2, 1)
                        e_l2.done(eng.tensor_tensor(l_st[st], l_st[st], ls[par], ALU.add))
                        o3 = o_st[st][:, :].rearrange("p (h d) -> p h d", h=NH)
                        e_osc.done(eng.tensor_tensor(o3, o3, al.unsqueeze(2).broadcast_to((P, NH, HD)), ALU.mult))
                    if end and h == 5:
                        e_ot.wait(eng, s - 2, 1)
                        e_osc.wait(eng, s - 2, 1)
                        e_oadd.done(eng.tensor_tensor(o_st[st][:, :], ps_t[:, :], o_st[st][:, :], ALU.add))
                    j = h // 2 - 2
                    if proj and h % 2 == 0 and 0 <= j < GT:
                        e_khi.wait(eng, s, j + 1)
                        part = slice(j * P, (j + 1) * P)
                        e_klo.done(eng.tensor_tensor(kt_lo[:, :, part], ps_t[:, :].rearrange("p (c k) -> p c k", c=DC),
                                                     kt_hi[:, :, part].bitcast(F32), ALU.subtract))
                if score:
                    e_nm.wait(eng, g, NH)
                    old = nm_init if (not loop and s in (1, 2)) else nm[par]
                    if loop or s >= 2:
                        e_al.wait(eng, g, 0)
                    e_dm.done(eng.tensor_tensor(dm, nm[1 - par], old, ALU.subtract))

            steps(eng, step)
            e_oadd.wait(eng, NG - 1, 1)
            e_l2.wait(eng, NG - 1, 1)
            o3 = [o[:, :].rearrange("p (h d) -> p h d", h=NH) for o in o_st]
            for i in range(2):
                chain(eng.reciprocal(rl, l_st[i]))
                chain(eng.tensor_tensor(o3[i], o3[i], rl.unsqueeze(2).broadcast_to((P, NH, HD)), ALU.mult))
                chain(eng.tensor_tensor(o_st[i][:, :], o_st[i][:, :], o_rows[:, 1 + (1 - i), :], ALU.add))
            e_osum.done(eng.tensor_tensor(o_st[0][:, :], o_st[0][:, :], o_st[1][:, :], ALU.add))
            e_pe.wait(eng, 0, 6)
            chain(eng.tensor_tensor(xn[:, :], ps_a[0][:, :], o_rows[:, 0, :], ALU.add))
            e_x1.done(eng.tensor_tensor(x1[:, :], xn[:, :], x_sb[:, :], ALU.add))
            e_x1.wait(eng, 0, 1)

            layernorm(yn[:, :], x1[:, :], e_ln)
            for i in range(3):
                dst = (sq, sk, sv)[i]
                e_codes[i].wait(eng, 0, 1)
                for c in range(DC):
                    scale = ring_loaded(eng, i * (DC + 1) + c)
                    e_deq.done(eng.tensor_tensor(codes[i][:, c, :], codes[i][:, c, :], scale[:, :], ALU.mult))
                bias = ring_loaded(eng, i * (DC + 1) + DC)
                for b in range(NB):
                    n = slice(b * 512, (b + 1) * 512)
                    e_pj.wait(eng, 0, NB * i + b + 1)
                    e_pjb.done(eng.tensor_tensor(dst[:, n], ps_pj[b % 2][:, :], bias[:, n], ALU.add))
            for b in range(NB):
                bank = ps_sc[b][:, :].rearrange("p (h k) -> p h k", h=HB)
                hs = slice(b * HB, (b + 1) * HB)
                e_ss.wait(eng, 0, b + 1)
                chain(eng.tensor_reduce(s_max[:, hs], bank, AX.X, ALU.max))
                e_smax.done(eng.tensor_scalar(s_nb[:, hs], s_max[:, hs], -SD ** -0.5, None, ALU.mult))
            for b in range(NB):
                hs = slice(b * HB, (b + 1) * HB)
                e_sexp.wait(eng, 0, (b + 1) * HB)
                chain(eng.reciprocal(s_rec[:, hs], s_sum[:, hs]))
                part = sp[:, b * 512:(b + 1) * 512].rearrange("p (h k) -> p h k", h=HB)
                e_sn.done(eng.tensor_tensor(part, part, s_rec[:, hs].unsqueeze(2).broadcast_to((P, HB, P)), ALU.mult))
            e_codes[3].wait(eng, 0, 1)
            for b in range(NB):
                scale = ring_loaded(eng, 3 * (DC + 1) + b)
                part = codes_o[:, b * HB:(b + 1) * HB, :]
                e_deq.done(eng.tensor_tensor(part, part, scale[:, :].rearrange("p (c f) -> p c f", c=HB), ALU.mult))
            e_bo.wait(eng, 0, 1)
            chain(eng.tensor_tensor(x1[:, :], x1[:, :], bo_row[:, :], ALU.add))
            e_sf.wait(eng, 0, 1)
            e_x2.done(eng.tensor_tensor(x2[:, :], ps_pj[0][:, :], x1[:, :], ALU.add))
            e_x2.wait(eng, 0, 1)

            layernorm(x3[:, :], x2[:, :], e_ln)
            e_gate.wait(eng, 0, 2)
            e_tri.wait(eng, 0, 1)
            e_lge.wait(eng, 0, 1)
            chain(eng.tensor_scalar(score, score, 1.0, None, ALU.add))
            chain(eng.reciprocal(score, score))
            chain(eng.tensor_tensor(sc, score, gate_b[:, :], ALU.add))
            for i in range(NGRP):
                chain(eng.max(top8[:, i, :], sc[:, i * GE:(i + 1) * GE]))
            chain(eng.tensor_tensor(gs, top8[:, :, 0], top8[:, :, 1], ALU.add))

            def ranks(dst, v, n):
                other = v.unsqueeze(1).broadcast_to((P, n, n))
                own = v.unsqueeze(2).broadcast_to((P, n, n))
                a, b = cmp_a[:, 0:n, 0:n], cmp_b[:, 0:n, 0:n]
                chain(eng.tensor_tensor(a, other, own, ALU.is_gt))
                chain(eng.tensor_tensor(b, other, own, ALU.is_equal))
                chain(eng.tensor_tensor(b, b, earlier[:, 0:n, 0:n], ALU.mult))
                chain(eng.tensor_tensor(a, a, b, ALU.add))
                chain(eng.tensor_reduce(dst, a, AX.X, ALU.add))

            ranks(grank, gs, NGRP)
            chain(eng.tensor_scalar(gmask, grank, float(TOPG), None, ALU.is_lt))
            chain(eng.tensor_tensor(tmp.rearrange("p (g e) -> p g e", g=NGRP), sc.rearrange("p (g e) -> p g e", g=NGRP),
                                    gmask.unsqueeze(2).broadcast_to((P, NGRP, GE)), ALU.mult))
            ranks(rank, tmp, NE)
            chain(eng.tensor_scalar(sel, rank, float(TOPK), None, ALU.is_lt))
            chain(eng.tensor_tensor(gw, score, sel, ALU.mult))
            chain(eng.tensor_reduce(wsum, gw, AX.X, ALU.add))
            chain(eng.tensor_scalar(wsum, wsum, 1e-20, None, ALU.add))
            chain(eng.reciprocal(wrec, wsum))
            e_gw.done(eng.tensor_scalar(gw, gw, wrec, RSCALE, ALU.mult, ALU.mult))
            e_gw.wait(eng, 0, 1)

            e_sge.wait(eng, 0, 1)
            chain(eng.tensor_scalar(sh_e[:, :], sh_e[:, :], 1.0, None, ALU.add))
            chain(eng.reciprocal(sh_e[:, :], sh_e[:, :]))
            chain(eng.tensor_tensor(sh_a[:, :], ps_sg[:, :], sh_e[:, :], ALU.mult))
            e_shh.done(eng.tensor_tensor(sh_h[:, :], ps_su[:, :], sh_a[:, :], ALU.mult))

            with eng.Fori(0, NE // NR) as k:
                e_gc.done(eng.tensor_copy(g_col[:, :], gw[:, bass.ds(k * NR, NR)]))
                e_gc.wait(eng, k, 1)
                for i in range(NR):
                    m = m_e[i % 2][:, :]
                    e_he.wait(eng, k, i + 1)
                    e_m1.done(eng.tensor_scalar(m, m, 1.0, None, ALU.add))
                    e_m1.wait(eng, k, i + 1)
                    e_m2.done(eng.reciprocal(m, m))
                    e_m2.wait(eng, k, i + 1)
                    e_m3.done(eng.scalar_tensor_tensor(m, ps_h[i % 2][:, 0:NF], g_col[:, i:i + 1], m, ALU.mult, ALU.mult))
                    e_m3.wait(eng, k, i + 1)
                    e_hid.done(eng.tensor_tensor(m_h[i % 2][:, :], ps_h[i % 2][:, NF:2 * NF], m, ALU.mult))
            e_yd.wait(eng, 0, 1)
            e_fin.done(eng.tensor_tensor(y_out[:, :], ps_y[:, :], x2[:, :], ALU.add))

        @block.tensor
        def _(eng):
            def transposes(dst, src):
                for c in range(4):
                    last = eng.transpose(dst[:, c * P:(c + 1) * P], src[:, c * P:(c + 1) * P], ident[:, :])
                return last

            def split_product(dst, a, b, lo, hi):
                steps = [(x, y) for (a_hi, a_lo), (b_hi, b_lo) in zip(a, b) for x, y in ((a_hi, b_hi), (a_hi, b_lo), (a_lo, b_hi))]
                for k in range(lo, hi):
                    last = eng.matmul(dst, *steps[k], start=(k == 0), stop=(k == len(steps) - 1))
                return last

            e_pool.wait(eng, 0, 2)
            e_dve.wait(eng, 0, 2)
            e_pe.done(transposes(ps_t, xn))
            e_act.wait(eng, 0, 1)
            e_wq.wait(eng, 0, 1)
            for c in range(DC):
                last = eng.matmul(ps_a[0][:, :], xnt[:, c * P:(c + 1) * P], wq[:, c, :], start=(c == 0), stop=(c == DC - 1))
            e_pe.done(last)
            for i in range(2):
                e_dve.wait(eng, 0, 5 + 5 * i)
                e_pe.done(transposes(ps_t, qf))
            e_wlo.wait(eng, 0, 2)

            def step(eng, s, par, loop=False):
                proj, score, end = parts(s, loop)
                g = s - 1
                wi = 0 if (not loop and s == 0) else 2
                qi = 0 if (not loop and s == 1) else 1
                if not loop and s == 1:
                    e_dve.wait(eng, 0, 14)
                    e_wlo.wait(eng, 0, 4)
                for h in range(NH):
                    if score:
                        if h == 0:
                            e_stk.wait(eng, g, 1)
                        if loop or g > 0 or h >= NS:
                            e_exp.wait(eng, g, h + 1 - NS)
                        e_qk.done(eng.matmul(ps_s[h % NS][:, :], q_st[qi][0:NST * HD, h, :], stk[1 - par][0:NST * HD, h, :],
                                             start=True, stop=True))
                    if proj:
                        u, half = divmod(h, 2)
                        i, j = divmod(u, GT)
                        if half == 0:
                            if i == 0:
                                e_clo.wait(eng, s, j + 1)
                            if u >= 2 + GT:
                                e_v.wait(eng, s, u - 1 - GT)
                            elif u >= 2:
                                e_kb.wait(eng, s, u - 1)
                            elif loop or s > 0:
                                e_v.wait(eng, s, u - 1)
                        part = slice(j * P, (j + 1) * P)
                        halves = [(cx_hi[:, k, part], cx_lo[:, k, part]) for k in range(DC)]
                        w = [(w_hi[wi + i][:, k, :], w_lo[wi + i][:, k, :]) for k in range(DC)]
                        n = 3 * DC // 2
                        last = split_product(ps_a[u % 2][:, :], halves, w, half * n, (half + 1) * n)
                        if half:
                            (e_kp, e_vp)[i].done(last)
                    gp, hp = (g, h - 2) if h >= 2 else (g - 1, h - 2 + NH)
                    if (score and h >= 2) or (end and h < 2):
                        e_exp.wait(eng, gp, hp + 1)
                        if loop or s >= 2 or h > 3:
                            e_pte.wait(eng, gp, hp - 1)
                        e_pt.done(transposes(ps_pt[hp % 2], p_sb[hp % NP]))
                    j = h // 2 - 2
                    if proj and h % 2 == 0 and 0 <= j < GT:
                        e_kn.wait(eng, s, j + 1)
                        if j == 1 and end:
                            e_oadd.wait(eng, s - 2, 1)
                        if loop or s > 0 or j > 0:
                            e_klo.wait(eng, s, j)
                        e_kt.done(transposes(ps_t, kn[j % 2]))
                    gp, hp = (g, h - 3) if h >= 3 else (g - 1, h - 3 + NH)
                    if (score and h >= 3) or (end and h < 3):
                        e_pte.wait(eng, gp, hp + 1)
                        if h == 3:
                            e_v.wait(eng, g, GT)
                            if loop or g > 0:
                                e_oc.wait(eng, g, 0)
                        cp, jp = hp // HC, hp % HC
                        vb = v_sb[1 - par] if h >= 3 else v_sb[par]
                        for k in range(GT):
                            last = eng.matmul(ps_o[jp * HD:(jp + 1) * HD, cp * P:(cp + 1) * P],
                                              vb[:, k, hp * HD:(hp + 1) * HD], pt_sb[hp % 2][:, k * P:(k + 1) * P],
                                              start=(k == 0), stop=(k == GT - 1))
                        e_pv.done(last)
                    if end and h == 5:
                        e_oc.wait(eng, s - 2, 1)
                        if proj:
                            e_klo.wait(eng, s, 1)
                        e_ot.done(transposes(ps_t, ot_sb))

            steps(eng, step)
            e_osum.wait(eng, 0, 1)
            e_pe.done(transposes(ps_t, o_st[0]))
            e_act.wait(eng, 0, 2 + 4 * HC + 1)
            e_wo.wait(eng, 0, 1)
            for c in range(DC):
                last = eng.matmul(ps_a[0][:, :], xnt[:, c * P:(c + 1) * P], wo[:, c, :], start=(c == 0), stop=(c == DC - 1))
            e_pe.done(last)

            e_ln.wait(eng, 0, 1)
            e_lnt.done(transposes(ps_t, yn))
            e_lntc.wait(eng, 0, 1)
            for i in range(3):
                e_deq.wait(eng, 0, DC * (i + 1))
                for b in range(NB):
                    if NB * i + b >= 2:
                        e_pjb.wait(eng, 0, NB * i + b - 1)
                    for c in range(DC):
                        last = eng.matmul(ps_pj[b % 2][:, :], ynt[:, c * P:(c + 1) * P],
                                          codes[i][:, c, b * 512:(b + 1) * 512], start=(c == 0), stop=(c == DC - 1))
                    e_pj.done(last)
                if i:
                    for b in range(NB):
                        n = NB * (i - 1) + b
                        e_pjb.wait(eng, 0, n + 1)
                        if n >= 2:
                            e_trc.wait(eng, 0, n - 1)
                        e_tr.done(transposes(ps_tr[b % 2], (sq, sk)[i - 1][:, b * 512:(b + 1) * 512]))
            e_trc.wait(eng, 0, 2 * NB)
            for b in range(NB):
                for h in range(b * HB, (b + 1) * HB):
                    part = slice(h * P, (h + 1) * P)
                    last = eng.matmul(ps_sc[b][:, (h % HB) * P:(h % HB + 1) * P], sqt[:, part], skt[:, part], start=True, stop=True)
                e_ss.done(last)
            for b in range(NB + 1):
                if b < NB:
                    e_sn.wait(eng, 0, b + 1)
                    if b >= 2:
                        e_sptc.wait(eng, 0, b - 1)
                    e_spt.done(transposes(ps_tr[b % 2], sp[:, b * 512:(b + 1) * 512]))
                if b:
                    e_sptc.wait(eng, 0, b)
                    for h in range((b - 1) * HB, b * HB):
                        part = slice(h * P, (h + 1) * P)
                        last = eng.matmul(ps_sc[b - 1][:, (h % HB) * P:(h % HB + 1) * P], sv[:, part], spt[:, part], start=True, stop=True)
                    e_so.done(last)
            e_soc.wait(eng, 0, NB)
            e_deq.wait(eng, 0, 3 * DC + NB)
            for h in range(SH):
                last = eng.matmul(ps_pj[0][:, :], sot[:, h * P:(h + 1) * P], codes_o[:, h, :], start=(h == 0), stop=(h == SH - 1))
            e_sf.done(last)

            e_ln.wait(eng, 0, 2)
            e_lnt.done(transposes(ps_t, x3))
            e_lntc.wait(eng, 0, 2)
            e_gate.wait(eng, 0, 2)

            def times_x3(dst, w):
                for c in range(DC):
                    last = eng.matmul(dst, x3t[:, c * P:(c + 1) * P], w[:, c, :], start=(c == 0), stop=(c == DC - 1))
                return last

            e_lg.done(times_x3(ps_lg[:, 0:NE], gate_w))
            e_shw.wait(eng, 0, 3)
            e_sg.done(times_x3(ps_sg[:, :], sh_w[0]))
            e_sg.done(times_x3(ps_su[:, :], sh_w[1]))
            e_shh.wait(eng, 0, 1)
            e_sht.done(transposes(ps_t, sh_h))
            e_shtc.wait(eng, 0, 1)

            def shared_down(c):
                return eng.matmul(ps_y[:, :], sh_ht[:, c * P:(c + 1) * P], sh_w[2][:, c, :], start=(c == 0), stop=(c == DC - 1),
                                  skip_group_check=True)

            def expert_up(k, i):
                e_ew[i % NR].wait(eng, k + i // NR, 1)
                if not isinstance(k, int) or k * NR + i > 1:
                    e_hid.wait(eng, k, i - 1)
                e_h.done(times_x3(ps_h[i % 2][:, :], w13[i % NR]))

            def expert_down(k, i):
                e_hid.wait(eng, k, i + 1)
                for c in range(NF // P):
                    last = eng.transpose(ps_ht[i % 2][:, c * P:(c + 1) * P], m_h[i % 2][:, c * P:(c + 1) * P], ident[:, :])
                e_ht.done(last)
                e_htc.wait(eng, k, i + 1)
                for c in range(NF // P):
                    last = eng.matmul(ps_y[:, :], m_ht[i % 2][:, c * P:(c + 1) * P], w2[i][:, c, :], start=False, stop=False,
                                      skip_group_check=True)
                e_y.done(last)

            def experts(k, final=False):
                for i in range(NR):
                    if not final or i + 1 < NR:
                        expert_up(k, i + 1)
                    expert_down(k, i)

            shared_down(0)
            expert_up(0, 0)
            experts(0)
            with eng.Fori(1, NE // NR - 1) as k:
                experts(k)
            experts(NE // NR - 1, final=True)
            for c in range(1, DC):
                last = shared_down(c)
            e_yd.done(last)


NAMES = ["q_b", "k_b", "v_b", "k_img_b", "v_img_b", "o_b", "norm_q_w", "norm_k_w", "norm_k_img_w"]


def kernel(**inputs):
    import numpy as np
    import concourse.bacc as bacc
    from concourse import mybir as mb
    from concourse.bass_utils import run_bass_kernel_spmd as run

    def lay(a):
        return np.ascontiguousarray(np.asarray(a))

    arrays = {"x": lay(inputs["x"][0]), "ctx_t": lay(np.asarray(inputs["ctx_2048"])[0].T)}
    for n in NAMES:
        arrays[n] = lay(inputs["L0_xattn_" + n])
    for n in ["q", "k", "v", "k_img", "v_img", "o"]:
        arrays[n + "_wt"] = lay(np.asarray(inputs[f"L0_xattn_{n}_w"]).T)
    for n in "qkvo":
        for part in ("codes", "scales"):
            arrays[f"w{n}_{part}"] = lay(inputs[f"L0_attn_w{n}_{part}"])
        arrays["b" + n] = lay(inputs["L0_attn_b" + n])
    for n in ("w1", "w2", "w3", "gate_bias", "shared_gate", "shared_up", "shared_down"):
        arrays[n] = lay(inputs["L0_ffn_" + n])
    arrays["gate_wt"] = lay(np.asarray(inputs["L0_ffn_gate_w"]).T)
    nc = bacc.Bacc("TRN2", target_bir_lowering=False, num_devices=1)
    t = {n: nc.dram_tensor(n, a.shape, mb.dt.from_np(a.dtype), kind="ExternalInput").ap() for n, a in arrays.items()}
    out = nc.dram_tensor("out", (P, D), mb.dt.float32, kind="ExternalOutput").ap()
    program(nc, t, out)
    r = run(nc, [arrays], core_ids=[0])
    return r.results[0]["out"].reshape(1, P, D)
```

```python
import concourse.bass as bass
from concourse import mybir
from contextlib import ExitStack

F32 = mybir.dt.float32
F32R = mybir.dt.float32r
ALU = mybir.AluOpType
ACT = mybir.ActivationFunctionType
AX = mybir.AxisListType

P = 128
D = 512
DC = D // P
NH, HD = 16, 32
HC = P // HD
NK = 12544
IMG = 257
GK = 512
GT = GK // P
TXT0 = IMG - 1
NG = 1 + (NK - TXT0) // GK
assert TXT0 + (NG - 1) * GK == NK and IMG <= GK
SH, SD = 16, 128
SF = SH * SD
HB = 4
NB = SH // HB
QB = 32
NE, NF = 32, 256
NGRP, TOPG, TOPK = 4, 2, 4
GE = NE // NGRP
FS = 512
RSCALE = 2.0
BIG = 3.0e38
LN_EPS, RMS_EPS = 1e-5, 1e-6


class Event:

    def __init__(self, sem, per=0, by=1):
        self.sem, self.per, self.by, self.n = sem, per, by, 0

    def done(self, ins):
        ins.then_inc(self.sem, self.by)
        self.n += 1
        return self.n

    def part(self, ins):
        ins.then_inc(self.sem, 16)

    def wait(self, eng, rnd, n):
        eng.wait_ge(self.sem, (rnd * self.per + n) * self.by)


def program(nc, t, out):
    ctx = ExitStack()
    with ctx:
        base = (nc.sbuf_base + 31) // 32 * 32
        KB = 1024
        ctx.enter_context(nc.sbuf_tensor("arena", [P, 207 * KB // 4 + 128], F32))

        def sb(name, off, shape, dt=F32):
            return nc.alloc_sbuf_tensor_at(name, shape, dt, offset=base + off)

        def event(name, per=0, by=1):
            return Event(ctx.enter_context(nc.semaphore(name)), per, by)

        W_NAMES = ["k_img", "v_img", "k", "v"]
        RAW_AT, W_AT = (0, 8, 136, 176), (64, 80, 0, 16)
        w_hi = [sb(f"w_hi_{n}", W_AT[i] * KB, [P, DC, D], F32R) for i, n in enumerate(W_NAMES)]
        w_lo = [sb(f"w_lo_{n}", (W_AT[i] + 8) * KB, [P, DC, D], F32R) for i, n in enumerate(W_NAMES)]
        stage = [sb(f"stage_{n}", RAW_AT[i] * KB, [P, DC, D]) for i, n in enumerate(W_NAMES)]
        wq = sb("wq", 16 * KB, [P, DC, D])
        q_rows = sb("q_rows", 24 * KB, [P, 4, D])
        NST = 3
        stk = [sb(f"k_stack{i}", (32 + 32 * i) * KB, [P, NH, GK], F32R) for i in range(2)]
        q_st = [sb(f"q_stack{i}", (96 + 8 * i) * KB, [P, NH, P], F32R) for i in range(2)]
        kt_hi, kt_lo = sb("kt_hi", 112 * KB, [P, DC, GK], F32R), sb("kt_lo", 120 * KB, [P, DC, GK], F32R)
        v_sb = [sb(f"v_sb{i}", (128 + 8 * i) * KB, [P, GT, D]) for i in range(2)]
        cx = sb("cx", 144 * KB, [P, DC, GK])
        cx_hi, cx_lo = sb("cx_hi", 152 * KB, [P, DC, GK], F32R), sb("cx_lo", 160 * KB, [P, DC, GK], F32R)
        kb = [sb(f"kb{i}", (168 + 2 * i) * KB, [P, D]) for i in range(2)]
        squares = sb("squares", 172 * KB, [P, D])
        NP = 4
        p_sb = [sb(f"p{i}", (176 + 2 * i) * KB, [P, GK]) for i in range(NP)]
        PT_AT = (184, 186, 188, 174, 198, 200, 202, 204)
        NPT = len(PT_AT)
        pt_sb = [sb(f"pt{i}", at * KB, [P, GK]) for i, at in enumerate(PT_AT)]
        k_bias = [sb(f"k_bias{i}", at * KB, [P, D]) for i, at in enumerate((200, 190))]
        ot_sb = sb("ot_sb", 192 * KB, [P, D])
        o_st = [sb(f"o_st{i}", (194 + 2 * i) * KB, [P, D]) for i in range(2)]
        x_sb = sb("x_sb", 198 * KB, [P, D])
        x_again = sb("x_again", 118 * KB, [P, D])
        o_rows = sb("o_rows", 112 * KB, [P, 3, D])
        ident = sb("ident", 206 * KB, [P, P])
        small = sb("small", 206 * KB + 512, [P, 256])
        cols = iter(range(0, 256, 16))
        nm = [small[:, c:c + NH] for c in (next(cols), next(cols))]
        nm_init, ngm, dm, al = (small[:, c:c + NH] for c in (next(cols), next(cols), next(cols), next(cols)))
        ls = [small[:, c:c + NH] for c in (next(cols), next(cols))]
        l_st = [small[:, c:c + NH] for c in (next(cols), next(cols))]
        c = next(cols)
        k_ss, k_r = small[:, c:c + GT], small[:, c + GT:c + 2 * GT]
        c = next(cols)
        stats, mv, rstd, q_ss, q_r = (small[:, c:c + 6], small[:, c + 6:c + 8], small[:, c + 8:c + 9],
                                      small[:, c + 9:c + 10], small[:, c + 10:c + 11])
        rl = small[:, 192:192 + NH]
        zero_col, ln_eps, rms_eps, minus_half = (small[:, i:i + 1] for i in range(208, 212))
        one_col = small[:, 221:222]
        k_t, r_t = small[:, 212:212 + GT], small[:, 220:221]
        wo = sb("wo", 96 * KB, [P, DC, D])
        xnt = kb[1]
        ln_x, ln_xt, q_sq = pt_sb[0], pt_sb[1], sb("q_sq", 202 * KB, [P, D])
        qf, qn = [ot_sb, sb("q_text", 204 * KB, [P, D])], sb("q_normed", 200 * KB, [P, D])
        p_tail = sb("p_tail", 176 * KB, [P, NP, GK])[:, :, IMG:]

        QKV = "qvk"
        codes = {n: sb(f"codes_{n}", off * KB, [P, DC, SF]) for n, off in (("q", 0), ("v", 64), ("k", 32))}
        codes_o = sb("codes_o", 96 * KB, [P, SH, D])
        NRING = 3
        ring = [sb(f"scale_ring{i}", (144 + 8 * i) * KB, [P, SF]) for i in range(NRING)]
        sq = sb("sq", 128 * KB, [P, SF])
        sqt = sb("sqt", 136 * KB, [P, SF])
        sk = sb("sk", 168 * KB, [P, SF])
        skt = sb("skt", 176 * KB, [P, SF])
        sv = sb("sv", 184 * KB, [P, SF])
        qkv = {"q": sq, "v": sv, "k": sk}
        sp, spt, sot = sq, sk, skt
        bo_row = sb("bo_row", 192 * KB, [P, D])
        x1 = sb("x1", 194 * KB, [P, D])
        yn, ynt = sb("yn", 198 * KB, [P, D]), sb("ynt", 200 * KB, [P, D])
        s_max, s_nb, s_sum, s_rec = (small[:, i:i + SH] for i in (0, 16, 32, 48))

        NR = 8
        SLOT_AT = (72, 84, 24, 36, 48, 60, 144, 156)
        w13 = [sb(f"w13_{i}", SLOT_AT[i] * KB, [P, DC, 2 * NF]) for i in range(NR)]
        w2 = [sb(f"w2_{i}", (SLOT_AT[i] + 8) * KB, [P, NF // P, D]) for i in range(NR)]
        w13_hi = [sb(f"w13_hi{i}", (96 + 8 * i) * KB, [P, DC, 2 * NF], F32R) for i in range(2)]
        w13_lo = [sb(f"w13_lo{i}", (112 + 8 * i) * KB, [P, DC, 2 * NF], F32R) for i in range(2)]
        x3t_hi, x3t_lo = (sb(f"x3t_{n}", at * KB, [P, D], F32R) for n, at in (("hi", 192), ("lo", 194)))
        sh_w = [sb(f"shared_{n}", 8 * i * KB, [P, DC, FS]) for i, n in enumerate(["gate", "up", "down"])]
        cmp_a = sb("cmp_a", 128 * KB, [P, NE, NE])
        cmp_b = sb("cmp_b", 132 * KB, [P, NE, NE])
        gate_w = sb("gate_w", 196 * KB, [P, DC, NE])
        gate_b = sb("gate_b", 196 * KB + 512, [P, NE])
        earlier = sb("earlier", 202 * KB, [P, NE, NE])
        rt = sb("router", 168 * KB, [P, 16, NE])
        sh_e, sh_a = sb("sh_e", 170 * KB, [P, FS]), sb("sh_a", 172 * KB, [P, FS])
        sh_h, sh_ht = sb("sh_h", 174 * KB, [P, FS]), sb("sh_ht", 176 * KB, [P, FS])
        m_e = [sb(f"m_e{i}", (178 + i) * KB, [P, NF]) for i in range(2)]
        m_h = [sb(f"m_h{i}", (180 + i) * KB, [P, NF]) for i in range(2)]
        m_ht = [sb(f"m_ht{i}", (182 + i) * KB, [P, NF]) for i in range(2)]
        g_col = sb("g_col", 184 * KB, [P, NR])
        x2 = sb("x2", 186 * KB, [P, D])
        x3, x3t = sb("x3", 188 * KB, [P, D]), sb("x3t", 190 * KB, [P, D])
        y_out = sb("y_out", 200 * KB, [P, D])
        score, sc, tmp, sel, gw, rank = (rt[:, i, :] for i in range(6))
        top8 = rt[:, 8, :].rearrange("p (g e) -> p g e", g=NGRP)
        gs, gmask, grank = (rt[:, 9 + i, 0:NGRP] for i in range(3))
        wsum, wrec = rt[:, 14, 0:1], rt[:, 15, 0:1]

        ps = [ctx.enter_context(nc.psum_tensor(f"ps{i}", [P, 512], F32)) for i in range(8)]
        ps_a, ps_t, ps_pt, ps_o = ps[0:2], ps[2], (ps[3], ps[7]), ps[4]
        ps_s = ps[5:7]
        NS = len(ps_s)

        e_x = event("x_loaded", by=16)
        e_wq = event("wq_loaded", by=16)
        e_kbias, e_qrows, e_orows = (event(n + "_rows_loaded", by=16) for n in ("k_bias", "q", "output"))
        e_w = [event(f"w_loaded_{n}", by=16) for n in W_NAMES]
        e_pool = event("pool_init")
        e_dve = event("dve_chain")
        e_lnx, e_lnxt, e_lnxc = event("x_normed"), event("x_normed_t"), event("x_normed_t_stored")
        e_qp, e_qb, e_qsq = event("q_projected"), event("q_biased"), event("q_squared")
        e_qh, e_qt, e_qst, e_qlo = event("q_scaled"), event("q_transposed"), event("q_stacked"), event("q_low_stacked")
        e_pz = event("p_tails_zeroed")
        e_at, e_atc, e_ap = event("attention_t"), event("attention_t_stored"), event("attention_projected")
        e_whi, e_wlo = event("w_hi_split"), event("w_lo_split")
        e_cx, e_cx0 = event("cx_loaded", 1, 16), event("first_tile_loaded", by=16)
        e_chi, e_clo = event("cx_hi", GT), event("cx_lo", GT)
        e_kp, e_vp = event("k_projected", GT), event("v_projected", GT)
        e_kb, e_sq, e_r, e_kn = event("k_biased", GT), event("k_squared", GT), event("k_rms", GT), event("k_normed", GT)
        e_kt, e_khi, e_klo, e_v = event("k_transposed", GT), event("kt_hi", GT), event("kt_lo", GT), event("v_stored", GT)
        HALVES = 2
        e_stk = event("keys_stacked", 1, 16 * HALVES * NST * HC)
        e_qk = event("scores", NH)
        e_gm, e_nm, e_exp = event("group_max", NH), event("running_max", NH), event("exp", NH)
        e_pt, e_pte, e_pv = event("p_transposed", NH), event("pt_stored", NH), event("pv_batch", NH // HC)
        e_dm, e_al, e_l1, e_l2 = event("max_step", 1), event("alpha", 1), event("l_scaled", 1), event("l_added", 1)
        e_osc, e_oc, e_ot, e_oadd = event("o_scaled", 1), event("ot_stored", 1), event("o_transposed", 1), event("o_added", 1)
        e_mask = event("masked", 1)
        e_wo = event("wo_loaded", by=16)
        e_osum, e_x1 = event("attention_summed"), event("x_after_cross")
        e_var, e_rs, e_rt = event("variance"), event("rsqrt"), event("k_mean_square", GT)
        e_out = event("out_stored", by=16)
        e_codes = {n: event(f"codes_loaded_{n}", by=16) for n in QKV + "o"}
        e_bias = {n: event(f"bias_loaded_{n}", by=16) for n in QKV}
        e_ring = [event(f"ring_loaded{i}", by=16 * P // QB) for i in range(NRING)]
        e_bo, e_deq = event("bo_loaded", by=16), event("dequantised")
        e_deqp = event("dequantised_by_pool")
        e_ln, e_lnt, e_lntc = event("normed"), event("normed_t"), event("normed_t_stored")
        e_pj, e_pjb = event("self_projected"), event("self_biased")
        e_tr, e_trc = event("self_transposed"), event("self_transposed_stored")
        e_ss, e_smax, e_sexp, e_sn = event("self_scores"), event("self_max"), event("self_exp"), event("self_normed")
        e_spt, e_sptc = event("self_p_transposed"), event("self_p_stored")
        e_so, e_soc = event("self_out"), event("self_out_stored")
        e_sf, e_x2 = event("self_final"), event("x_after_self")
        e_shw, e_gate = event("shared_loaded", by=16), event("gate_loaded", by=16)
        e_ew = [event(f"expert_loaded{i}", 1, 48) for i in range(NR)]
        e_lg, e_lge, e_gw = event("logits"), event("logits_exp"), event("gate_weights")
        e_tri = event("earlier_made")
        e_sg, e_sge, e_shh, e_sht, e_shtc = (event(n) for n in ("shared_h", "shared_exp", "shared_hidden",
                                                               "shared_t", "shared_t_stored"))
        e_h, e_he, e_hid, e_ht, e_htc, e_y = (event(n, NR) for n in ("expert_h", "expert_exp", "expert_hidden",
                                                                    "expert_t", "expert_t_stored", "expert_y"))
        e_gc = event("gate_columns", 1)
        e_x3hi, e_x3lo = event("x3_hi"), event("x3_lo")
        e_ehi, e_elo, e_elast = (event(n, NR) for n in ("expert_hi", "expert_lo", "expert_lo_last"))
        e_m1, e_m2, e_m3 = (event(n, NR) for n in ("expert_exp_plus1", "expert_sigmoid", "expert_gate"))
        e_yd, e_fin = event("y_done"), event("finished")

        ps_pj, ps_tr, ps_sc = ps[0:2], ps[2:4], ps[4:8]
        ps_lg, ps_sg, ps_su, ps_y, ps_h, ps_ht = ps[0], ps[1], ps[3], ps[4], ps[5:7], (ps[7], ps[2])

        def rows_of(ap):
            return ap.partition_broadcast(P)

        cxt = t["ctx_t"].rearrange("(c p) k -> p c k", p=P)

        def wview(ap):
            return ap.rearrange("(c p) o -> p c o", p=P)

        def steps(eng, step, peeled=0):
            step(eng, 0, 0)
            step(eng, 1, 1)
            step(eng, 2, 0)
            rounds = (NG - 3) // 2 - peeled
            with eng.Fori(0, rounds) as i:
                step(eng, i * 2 + 3, 1, loop=True)
                step(eng, i * 2 + 4, 0, loop=True)
            for s in range(3 + 2 * rounds, NG + 2):
                step(eng, s, s % 2)

        def parts(s, loop):
            return (loop or s < NG), (loop or 1 <= s <= NG), (loop or s >= 2)

        def mask(s, loop):
            if not loop and s == 1:
                return 0, IMG
            if not loop and s == 2:
                return 1, GK
            return 0, GK

        N_POOL = 2 + 2 + 1 + 1 + 2 + 4
        block = ctx.enter_context(nc.Block())
        SHARED_SLOT = NR - 2
        LC = DC - 1

        def split_low(eng, k, i, chunks, done):
            e_ehi.wait(eng, k, i + 1)
            done.done(eng.tensor_tensor(w13_lo[i % 2][:, chunks, :], w13[i % NR][:, chunks, :],
                                        w13_hi[i % 2][:, chunks, :].bitcast(F32), ALU.subtract))

        def rounds_of_experts(eng, one_round):
            with eng.Fori(0, NE // NR - 1) as k:
                one_round(k, NR)
            one_round(NE // NR - 1, NR - 2)


        def scales(n, c):
            return (QKV + "o").index(n) * DC + c

        NPOOL = DC + DC // 2

        def ring_free(eng, item):
            old = item - NRING
            if old >= NPOOL:
                e_deq.wait(eng, 0, old - NPOOL + 1)
            elif old >= 0:
                e_deqp.wait(eng, 0, old + 1)

        def ring_loaded(eng, item):
            e_ring[item % NRING].wait(eng, 0, item // NRING + 1)
            return ring[item % NRING]

        def dequantise(eng, n, c, done):
            e_codes[n].wait(eng, 0, c // (DC // 2) + 1 if n == "q" else 1)
            scale = ring_loaded(eng, scales(n, c))[:, :]
            part = codes_o[:, c * HB:(c + 1) * HB, :] if n == "o" else codes[n][:, c, :]
            if n == "o":
                scale = scale.rearrange("p (c f) -> p c f", c=HB)
            done.done(eng.tensor_tensor(part, part, scale, ALU.mult))

        @block.sync
        def _(eng):
            def load_weight(i):
                e_w[i].done(eng.dma_start(stage[i][:, :, :], wview(t[W_NAMES[i] + "_wt"])))

            load_weight(0)

            def load(g):
                if isinstance(g, int) and g == 0:
                    e_cx0.done(eng.dma_start(cx[:, :, 0:P], cxt[:, :, 0:P]))
                    e_cx.done(eng.dma_start(cx[:, :, P:GK], cxt[:, :, P:GK]))
                    return
                elif isinstance(g, int):
                    src = cxt[:, :, TXT0 + (g - 1) * GK:TXT0 + g * GK]
                else:
                    src = cxt[:, :, bass.ds(g * GK + (TXT0 - GK), GK)]
                e_cx.done(eng.dma_start(cx[:, :, :], src))

            load(0)
            for i, n in enumerate(["k_img_b", "k_b"]):
                e_kbias.done(eng.dma_start(k_bias[i][:, :], rows_of(t[n])))
            e_x.done(eng.dma_start(x_sb[:, :], t["x"]))
            load_weight(1)
            e_wq.done(eng.dma_start(wq[:, :, :], wview(t["q_wt"])))
            for i, n in enumerate(["q_b", "norm_q_w", "norm_k_img_w", "norm_k_w"]):
                e_qrows.done(eng.dma_start(q_rows[:, i, :], rows_of(t[n])))
            load_weight(2)
            load_weight(3)

            def step(eng, s, par, loop=False):
                if not loop and s >= NG:
                    return
                if loop or s < NG - 1:
                    e_clo.wait(eng, s, GT)
                    load(s + 1)
                if not loop and s == 1:
                    e_vp.wait(eng, 0, GT)
                for half in range(HALVES):
                    e_klo.wait(eng, s, (half + 1) * GT // HALVES)
                    if half == 0 and (loop or s >= 2):
                        e_qk.wait(eng, s - 2, NH)
                    keys = slice(half * GK // HALVES, (half + 1) * GK // HALVES)
                    for r, part in enumerate((kt_hi, kt_lo, kt_hi)):
                        for j in range(HC):
                            e_stk.part(eng.dma_start(stk[par][r * HD:(r + 1) * HD, j::HC, keys].bitcast(F32),
                                                     part[j * HD:(j + 1) * HD, :, keys].bitcast(F32)))
                if not loop and s == 1:
                    e_qk.wait(eng, 0, NH)
                    e_wo.done(eng.dma_start(wo[:, :, :], wview(t["o_wt"])))

            steps(eng, step, peeled=1)

            blocks = range(P // QB)

            def load_codes(n, half=None):
                dst, src = codes_o if n == "o" else codes[n], t[f"w{n}_codes"].rearrange("(c p) f -> p c f", p=P)
                part = slice(None) if half is None else slice(half * DC // 2, (half + 1) * DC // 2)
                e_codes[n].done(eng.dma_start(dst[:, part, :], src[:, part, :]))

            def load_scales(n, c):
                item = scales(n, c)
                ring_free(eng, item)
                for b in blocks:
                    rows = ring[item % NRING][b * QB:(b + 1) * QB, :]
                    if n == "o":
                        rows = rows.rearrange("p (c f) -> p c f", c=HB)
                        src = t["wo_scales"].rearrange("(c b) f -> b c f", b=len(blocks))[b, c * HB:(c + 1) * HB, :]
                    else:
                        src = t[f"w{n}_scales"][c * len(blocks) + b, :]
                    e_ring[item % NRING].part(eng.dma_start(rows, src.partition_broadcast(QB)))

            def load_bias(n):
                e_bias[n].done(eng.dma_start(qkv[n][:, :], rows_of(t["b" + n])))

            e_kp.wait(eng, 0, NG * GT)
            load_codes("q", 0)
            e_clo.wait(eng, 0, NG * GT)
            load_scales("q", 0)
            e_stk.wait(eng, 0, NG)
            for i, n in enumerate(["o_b", "v_b", "v_img_b"]):
                e_orows.done(eng.dma_start(o_rows[:, i, :], rows_of(t[n])))
            e_orows.done(eng.dma_start(x_again[:, :], t["x"]))
            e_vp.wait(eng, 0, NG * GT)
            load_codes("q", 1)
            for c in range(1, NRING):
                load_scales("q", c)
            e_qk.wait(eng, 0, (NG - 1) * NH)
            load_codes("v")
            load_scales("q", 3)
            load_scales("v", 0)
            load_scales("v", 1)
            e_pv.wait(eng, 0, NG * NH // HC)
            load_bias("q")
            load_scales("v", 2)
            load_scales("v", 3)
            load_bias("v")
            e_qk.wait(eng, 0, NG * NH)
            load_codes("k")
            e_x1.wait(eng, 0, 1)
            for c in range(DC):
                load_scales("k", c)
            load_bias("k")
            load_codes("o")
            for c in range(NB):
                load_scales("o", c)
            e_bo.done(eng.dma_start(bo_row[:, :], rows_of(t["bo"])))
            e_gate.done(eng.dma_start(gate_w[:, :, :], t["gate_wt"].rearrange("(c p) f -> p c f", p=P)))
            e_gate.done(eng.dma_start(gate_b[:, :], rows_of(t["gate_bias"])))
            e_pj.wait(eng, 0, NB)
            for i, n in enumerate(("gate", "up", "down")):
                e_shw.done(eng.dma_start(sh_w[i][:, :, :], t[f"shared_{n}"].rearrange("(c p) f -> p c f", p=P)))

            def load_expert(e, i):
                one = slice(e, e + 1) if isinstance(e, int) else bass.ds(e, 1)
                for half, n in enumerate(("w1", "w3")):
                    e_ew[i].part(eng.dma_start(w13[i][:, :, half * NF:(half + 1) * NF],
                                               t[n][one, :, :].rearrange("o (c p) f -> p (o c) f", p=P)))
                e_ew[i].part(eng.dma_start(w2[i][:, :, :], t["w2"][one, :, :].rearrange("o (c p) f -> p (o c) f", p=P)))

            for i in range(NR):
                if i < 2:
                    e_pj.wait(eng, 0, 2 * NB)
                elif i < 6:
                    e_pj.wait(eng, 0, 3 * NB)
                else:
                    e_deq.wait(eng, 0, 3 * DC + NB - NPOOL)
                load_expert(i, i)
            with eng.Fori(0, NE // NR - 1) as k:
                for i in range(NR):
                    e_y.wait(eng, k, i + 1)
                    load_expert(k * NR + (NR + i), i)
            e_fin.wait(eng, 0, 1)
            e_out.done(eng.dma_start(out, y_out[:, :]))
            e_out.wait(eng, 0, 1)

        @block.gpsimd
        def _(eng):
            eng.memset(ident[:, :], 0.0).then_inc(e_pool.sem, 1)
            e_pool.wait(eng, 0, 1)
            eng.affine_select(out=ident[:, :], in_=ident[:, :], compare_op=ALU.not_equal, fill=1.0,
                              base=0, pattern=[[-1, P]], channel_multiplier=1).then_inc(e_pool.sem, 1)
            for b in o_st:
                eng.memset(b[:, :], 0.0).then_inc(e_pool.sem, 1)
            eng.memset(zero_col, 0.0).then_inc(e_pool.sem, 1)
            eng.memset(nm_init, BIG).then_inc(e_pool.sem, 1)
            for l in l_st:
                eng.memset(l, 0.0).then_inc(e_pool.sem, 1)

            for v, x in ((ln_eps, LN_EPS), (rms_eps, RMS_EPS), (minus_half, -0.5), (one_col, 1.0)):
                eng.memset(v, x).then_inc(e_pool.sem, 1)
            e_pool.wait(eng, 0, N_POOL)

            def rsqrt(dst, src, eps):
                eng.tensor_tensor(r_t, src, eps, ALU.add).then_inc(e_pool.sem, 1)
                n_pool[0] += 1
                e_pool.wait(eng, 0, n_pool[0])
                e_rs.done(eng.tensor_tensor(dst, r_t, minus_half, ALU.pow))

            n_pool = [N_POOL]
            def key_norm(s, j):
                e_sq.wait(eng, s, j + 1)
                e_rt.done(eng.tensor_tensor(k_t[:, j:j + 1], k_ss[:, j:j + 1], rms_eps, ALU.add))
                e_rt.wait(eng, s, j + 1)
                e_r.done(eng.tensor_tensor(k_r[:, j:j + 1], k_t[:, j:j + 1], minus_half, ALU.pow))

            def step(eng, s, par, loop=False):
                proj, _, _ = parts(s, loop)
                if not proj:
                    return
                if not loop and s == 0:
                    e_cx0.wait(eng, 0, 1)
                else:
                    e_cx.wait(eng, s, 1)
                for j in range(GT):
                    if not loop and s == 0 and j == 1:
                        e_cx.wait(eng, 0, 1)
                    if not loop and s == 0 and j == 2:
                        e_var.wait(eng, 0, 1)
                        rsqrt(rstd, mv[:, 1:2], ln_eps)
                    part = slice(j * P, (j + 1) * P)
                    if loop or s > 0:
                        e_vp.wait(eng, s, j + 1 - GT)
                    e_chi.done(eng.tensor_tensor(cx_hi[:, :, part], cx[:, :, part],
                                                 one_col.unsqueeze(2).broadcast_to((P, DC, P)), ALU.mult))
                    e_chi.wait(eng, s, j + 1)
                    e_clo.done(eng.tensor_tensor(cx_lo[:, :, part], cx[:, :, part], cx_hi[:, :, part].bitcast(F32),
                                                 ALU.subtract))
                if not loop and s == 1:
                    e_wlo.wait(eng, 0, 4)
                    e_pz.done(eng.memset(p_tail, 0.0))
                for j in range(GT):
                    key_norm(s, j)
                if not loop and s == 0:
                    e_qsq.wait(eng, 0, 1)
                    rsqrt(q_r, q_ss, rms_eps)

            steps(eng, step)
            for c in range(DC):
                dequantise(eng, "q", c, e_deqp)
            e_var.wait(eng, 0, 2)
            rsqrt(rstd, mv[:, 1:2], ln_eps)
            for c in range(NPOOL - DC):
                dequantise(eng, "v", c, e_deqp)
            e_x1.wait(eng, 0, 1)
            eng.memset(earlier[:, :, :], 1.0).then_inc(e_pool.sem, 1)
            n_pool[0] += 1
            e_pool.wait(eng, 0, n_pool[0])
            e_tri.done(eng.affine_select(out=earlier[:, :, :], in_=earlier[:, :, :], compare_op=ALU.is_gt, fill=0.0,
                                         base=0, pattern=[[1, NE], [-1, NE]], channel_multiplier=0))
            e_var.wait(eng, 0, 3)
            rsqrt(rstd, mv[:, 1:2], ln_eps)
            for i in range(2):
                split_low(eng, 0, i, slice(0, LC), e_elo)
            def one_round(k, n):
                for i in range(n):
                    split_low(eng, k, i + 2, slice(0, LC), e_elo)

            rounds_of_experts(eng, one_round)

        @block.scalar
        def _(eng):
            copy, exp, square = ACT.Copy, ACT.Exp, ACT.Square
            def split_weight(i):
                e_w[i].wait(eng, 0, 1)
                e_whi.done(eng.activation(w_hi[i][:, :, :], stage[i][:, :, :], copy))

            split_weight(0)
            e_pool.wait(eng, 0, N_POOL)

            def stack_queries(i):
                e_qt.wait(eng, 0, i + 1)
                for j in range(HC):
                    head = ps_pt[i][j * HD:(j + 1) * HD, :].rearrange("p (c q) -> p c q", c=DC)
                    for r in range(2):
                        e_qst.done(eng.activation(q_st[i][r * HD:(r + 1) * HD, j::HC, :], head, copy))

            def prepare(h):
                if h == 2:
                    e_lnxt.wait(eng, 0, 1)
                    e_lnxc.done(eng.activation(ln_xt[:, :], ps_o[:, :], copy))
                if h == 3:
                    split_weight(1)
                if h == 8:
                    e_qb.wait(eng, 0, 1)
                    e_qsq.done(eng.activation(q_sq[:, :], qf[0][:, :], square, scale=D ** -0.5, accum_out=q_ss))
                if h == 6:
                    e_wlo.wait(eng, 0, 2)
                    split_weight(2)
                if h in (10, 11):
                    stack_queries(h - 10)
                if h == 9:
                    e_qp.wait(eng, 0, 1)
                    split_weight(3)

            def step(eng, s, par, loop=False):
                proj, score, end = parts(s, loop)
                g = s - 1
                lo, hi = mask(s, loop)
                for h in range(NH):
                    j = h // 2 - 1
                    if proj and h % 2 == 0 and 0 <= j < GT:
                        e_kb.wait(eng, s, j + 1)
                        e_sq.done(eng.activation(squares[:, :], kb[j % 2][:, :], square, scale=D ** -0.5,
                                                 accum_out=k_ss[:, j:j + 1]))
                    if score:
                        e_nm.wait(eng, g, h + 1)
                        if loop or g > 0 or h >= NP:
                            e_pt.wait(eng, g, h + 1 - NP)
                        if not loop and s == 1 and h == 0:
                            e_wlo.wait(eng, 0, 4)
                        pb = p_sb[h % NP]
                        if not loop and s == 2:
                            e_mask.done(eng.activation(pb[:, 0:1], zero_col, copy))
                        e_exp.done(eng.activation(pb[:, lo:hi], ps_s[h % NS][:, lo:hi], exp,
                                                  bias=nm[1 - par][:, h:h + 1], accum_out=ls[1 - par][:, h:h + 1]))
                    if end and h == 5:
                        e_pv.wait(eng, s - 2, NH // HC)
                        if loop or s > 2:
                            e_ot.wait(eng, s - 2, 0)
                        e_oc.done(eng.activation(ot_sb[:, :], ps_o[:, :], copy))
                    if proj and h % 2 == 0 and 0 <= j < GT:
                        e_r.wait(eng, s, j + 1)
                        e_kn.done(eng.activation(kb[j % 2][:, :], kb[j % 2][:, :], copy, scale=k_r[:, j:j + 1]))
                    j = h // 2 - 2
                    if proj and h % 2 == 0 and 0 <= j < GT:
                        e_kt.wait(eng, s, j + 1)
                        e_khi.done(eng.activation(kt_hi[:, :, j * P:(j + 1) * P],
                                                  ps_t[:, :].rearrange("p (c k) -> p c k", c=DC), copy))
                    j = h // 2 - GT
                    if proj and h % 2 == 1 and j >= 0:
                        e_vp.wait(eng, s, j + 1)
                        if loop or s >= 2:
                            e_pv.wait(eng, s - 2, NH // HC)
                        if not loop and s == 1 and j == 0:
                            e_wlo.wait(eng, 0, 3)
                        e_v.done(eng.activation(v_sb[par][:, j, :], ps_a[j % 2][:, :], copy))
                    if not loop and s == 0:
                        prepare(h)
                if score:
                    e_dm.wait(eng, g, 1)
                    if loop or g > 0:
                        e_osc.wait(eng, g, 0)
                    e_al.done(eng.activation(al, dm, exp))

            steps(eng, step)
            e_at.wait(eng, 0, 1)
            e_atc.done(eng.activation(xnt[:, :], ps_t[:, :], copy))

            e_lnt.wait(eng, 0, 1)
            e_lntc.done(eng.activation(ynt[:, :], ps_t[:, :], copy))
            for i, dst in enumerate((sqt, skt)):
                for b in range(NB):
                    e_tr.wait(eng, 0, NB * i + b + 1)
                    e_trc.done(eng.activation(dst[:, b * 512:(b + 1) * 512], ps_tr[b % 2][:, :], copy))
            for b in range(NB):
                e_smax.wait(eng, 0, b + 1)
                for i in range(HB):
                    h = b * HB + i
                    e_sexp.done(eng.activation(sp[:, h * P:(h + 1) * P], ps_sc[b][:, i * P:(i + 1) * P], exp,
                                               bias=s_nb[:, h:h + 1], scale=SD ** -0.5, accum_out=s_sum[:, h:h + 1]))
            for b in range(NB):
                e_spt.wait(eng, 0, b + 1)
                e_sptc.done(eng.activation(spt[:, b * 512:(b + 1) * 512], ps_tr[b % 2][:, :], copy))
                if b:
                    e_so.wait(eng, 0, b)
                    e_soc.done(eng.activation(sot[:, (b - 1) * 512:b * 512], ps_sc[b - 1][:, :], copy))
            e_so.wait(eng, 0, NB)
            e_soc.done(eng.activation(sot[:, (NB - 1) * 512:], ps_sc[NB - 1][:, :], copy))

            def split_high(k, i):
                e_ew[i % NR].wait(eng, k + i // NR, 1)
                e_ehi.done(eng.activation(w13_hi[i % 2][:, :, :], w13[i % NR][:, :, :], copy))

            e_sf.wait(eng, 0, 1)
            split_high(0, 0)
            e_lnt.wait(eng, 0, 2)
            e_lntc.done(eng.activation(x3t[:, :], ps_t[:, :], copy))
            e_x3hi.done(eng.activation(x3t_hi[:, :], ps_t[:, :], copy))
            e_lg.wait(eng, 0, 1)
            e_lge.done(eng.activation(score, ps_lg[:, 0:NE], exp, scale=-1.0))
            split_high(0, 1)
            e_sg.wait(eng, 0, 1)
            e_sge.done(eng.activation(sh_e[:, :], ps_sg[:, :], exp, scale=-1.0))

            def one_round(k, n):
                for i in range(NR):
                    e_h.wait(eng, k, i + 1)
                    e_he.done(eng.activation(m_e[i % 2][:, :], ps_h[i % 2][:, 0:NF], exp, scale=-1.0))
                    if i < n:
                        split_high(k, i + 2)
                    e_ht.wait(eng, k, i + 1)
                    e_htc.done(eng.activation(m_ht[i % 2][:, :], ps_ht[i % 2][:, 0:NF], copy))
                    if n < NR and i == SHARED_SLOT:
                        e_sht.wait(eng, 0, 1)
                        e_shtc.done(eng.activation(sh_ht[:, :], ps_lg[:, :], copy))

            rounds_of_experts(eng, one_round)

        @block.vector
        def _(eng):
            def chain(ins):
                n = e_dve.done(ins)
                e_dve.wait(eng, 0, n)
                return n

            n_rsqrt = iter((1, 3, 4))

            def layernorm(dst, src, done=None):
                chain(eng.bn_stats(stats, src))
                e_var.done(eng.bn_aggr(mv, stats))
                e_rs.wait(eng, 0, next(n_rsqrt))
                last = eng.tensor_scalar(dst, src, mv[:, 0:1], rstd, ALU.subtract, ALU.mult)
                return chain(last) if done is None else done.done(last)

            def split_weight(i):
                e_whi.wait(eng, 0, i + 1)
                e_wlo.done(eng.tensor_tensor(w_lo[i][:, :, :], stage[i][:, :, :], w_hi[i][:, :, :].bitcast(F32),
                                             ALU.subtract))

            split_weight(0)
            e_kbias.wait(eng, 0, 2)
            e_pool.wait(eng, 0, N_POOL)

            def prepare(h):
                if h == 0:
                    e_x.wait(eng, 0, 1)
                    layernorm(ln_x[:, :], x_sb[:, :], e_lnx)
                if h == 4:
                    split_weight(1)
                if h == 7:
                    e_qrows.wait(eng, 0, 4)
                    e_qp.wait(eng, 0, 1)
                    e_qb.done(eng.tensor_tensor(qf[0][:, :], ps_s[0][:, :], q_rows[:, 0, :], ALU.add))
                if h == 9:
                    e_rs.wait(eng, 0, 2)
                    chain(eng.scalar_tensor_tensor(qn[:, :], qf[0][:, :], q_r, q_rows[:, 1, :], ALU.mult, ALU.mult))
                    for i in range(2):
                        e_qh.done(eng.scalar_tensor_tensor(qf[i][:, :], qn[:, :], HD ** -0.5, q_rows[:, 2 + i, :],
                                                           ALU.mult, ALU.mult))
                if h in (11, 12):
                    i = h - 11
                    e_qst.wait(eng, 0, 2 * HC * (i + 1))
                    for j in range(HC):
                        e_qlo.done(eng.tensor_tensor(q_st[i][2 * HD:3 * HD, j::HC, :],
                                                     ps_pt[i][j * HD:(j + 1) * HD, :].rearrange("p (c q) -> p c q", c=DC),
                                                     q_st[i][0:HD, j::HC, :].bitcast(F32), ALU.subtract))
                if h in (10, 12):
                    e_qh.wait(eng, 0, 2)
                    split_weight(h // 2 - 3)

            def by_head(o):
                return o[:, :].rearrange("p (h d) -> p h d", h=NH)

            def image_part():
                e_orows.wait(eng, 0, 4)
                chain(eng.reciprocal(rl, l_st[0]))
                chain(eng.tensor_tensor(by_head(o_st[0]), by_head(o_st[0]), rl.unsqueeze(2).broadcast_to((P, NH, HD)), ALU.mult))
                for i in (1, 2):
                    chain(eng.tensor_tensor(o_st[0][:, :], o_st[0][:, :], o_rows[:, i, :], ALU.add))
                chain(eng.tensor_tensor(x_again[:, :], x_again[:, :], o_rows[:, 0, :], ALU.add))

            def step(eng, s, par, loop=False):
                proj, score, end = parts(s, loop)
                g = s - 1
                lo, hi = mask(s, loop)
                st = 0 if (not loop and s == 2) else 1
                for h in range(NH):
                    if not loop and s == NG + 1 and h == 3:
                        image_part()
                    if score:
                        old = nm_init if (not loop and s in (1, 2)) else nm[par]
                        e_qk.wait(eng, g, h + 1)
                        e_gm.done(eng.tensor_reduce(ngm[:, h:h + 1], ps_s[h % NS][:, lo:hi], AX.X, ALU.max, negate=True))
                        e_gm.wait(eng, g, h + 1)
                        e_nm.done(eng.tensor_tensor(nm[1 - par][:, h:h + 1], ngm[:, h:h + 1], old[:, h:h + 1], ALU.min))
                    gp, hp = (g, h - 2) if h >= 2 else (g - 1, h - 2 + NH)
                    if (score and h >= 2) or (end and h < 2):
                        e_pt.wait(eng, gp, hp + 1)
                        if loop or s >= 2 or hp >= NPT:
                            e_pv.wait(eng, gp, (hp - NPT) // HC + 1)
                        e_pte.done(eng.tensor_copy(pt_sb[hp % NPT][:, :], ps_pt[hp % 2][:, :]))
                    j = h // 2
                    if proj and h % 2 == 1 and j < GT:
                        e_kp.wait(eng, s, j + 1)
                        if loop or s > 0 or j >= 2:
                            e_kt.wait(eng, s, j + 1 - 2)
                        bias = k_bias[0 if (not loop and s == 0) else 1][:, :]
                        e_kb.done(eng.tensor_tensor(kb[j % 2][:, :], ps_a[j % 2][:, :], bias, ALU.add))
                    if end and h == 1:
                        e_al.wait(eng, s - 2, 1)
                        if loop or s > 2:
                            e_l2.wait(eng, s - 2, 0)
                            e_oadd.wait(eng, s - 2, 0)
                        e_l1.done(eng.tensor_tensor(l_st[st], l_st[st], al, ALU.mult))
                        e_exp.wait(eng, s - 2, NH)
                        e_l1.wait(eng, s - 2, 1)
                        e_l2.done(eng.tensor_tensor(l_st[st], l_st[st], ls[par], ALU.add))
                        o3 = o_st[st][:, :].rearrange("p (h d) -> p h d", h=NH)
                        e_osc.done(eng.tensor_tensor(o3, o3, al.unsqueeze(2).broadcast_to((P, NH, HD)), ALU.mult))
                    if end and h == 13:
                        e_ot.wait(eng, s - 2, 1)
                        e_osc.wait(eng, s - 2, 1)
                        e_oadd.done(eng.tensor_tensor(o_st[st][:, :], ps_t[:, :], o_st[st][:, :], ALU.add))
                    j = h // 2 - 2
                    if proj and h % 2 == 0 and 0 <= j < GT:
                        e_khi.wait(eng, s, j + 1)
                        part = slice(j * P, (j + 1) * P)
                        e_klo.done(eng.tensor_tensor(kt_lo[:, :, part], ps_t[:, :].rearrange("p (c k) -> p c k", c=DC),
                                                     kt_hi[:, :, part].bitcast(F32), ALU.subtract))
                    if not loop and s == 0:
                        prepare(h)
                if score:
                    e_nm.wait(eng, g, NH)
                    old = nm_init if (not loop and s in (1, 2)) else nm[par]
                    if loop or s >= 2:
                        e_al.wait(eng, g, 0)
                    e_dm.done(eng.tensor_tensor(dm, nm[1 - par], old, ALU.subtract))

            steps(eng, step)
            e_oadd.wait(eng, NG - 1, 1)
            e_l2.wait(eng, NG - 1, 1)
            chain(eng.reciprocal(rl, l_st[1]))
            chain(eng.tensor_tensor(by_head(o_st[1]), by_head(o_st[1]), rl.unsqueeze(2).broadcast_to((P, NH, HD)), ALU.mult))
            e_osum.done(eng.tensor_tensor(o_st[0][:, :], o_st[0][:, :], o_st[1][:, :], ALU.add))
            e_ap.wait(eng, 0, 1)
            e_x1.done(eng.tensor_tensor(x1[:, :], ps_a[0][:, :], x_again[:, :], ALU.add))
            e_x1.wait(eng, 0, 1)

            layernorm(yn[:, :], x1[:, :], e_ln)

            def add_bias(n, b):
                part = qkv[n][:, b * 512:(b + 1) * 512]
                e_bias[n].wait(eng, 0, 1)
                e_pj.wait(eng, 0, NB * QKV.index(n) + b + 1)
                e_pjb.done(eng.tensor_tensor(part, ps_pj[b % 2][:, :], part, ALU.add))

            for b in range(NB):
                add_bias("q", b)
                if b < NB - 1 and NPOOL - DC + b < DC:
                    dequantise(eng, "v", NPOOL - DC + b, e_deq)
            for b in range(NB):
                add_bias("v", b)
                dequantise(eng, "k", b, e_deq)
            for b in range(NB):
                add_bias("k", b)
            for c in range(NB // 2):
                dequantise(eng, "o", c, e_deq)
            for b in range(NB):
                bank = ps_sc[b][:, :].rearrange("p (h k) -> p h k", h=HB)
                hs = slice(b * HB, (b + 1) * HB)
                e_ss.wait(eng, 0, b + 1)
                chain(eng.tensor_reduce(s_max[:, hs], bank, AX.X, ALU.max))
                e_smax.done(eng.tensor_scalar(s_nb[:, hs], s_max[:, hs], -SD ** -0.5, None, ALU.mult))
            for b in range(NB):
                hs = slice(b * HB, (b + 1) * HB)
                e_sexp.wait(eng, 0, (b + 1) * HB)
                chain(eng.reciprocal(s_rec[:, hs], s_sum[:, hs]))
                part = sp[:, b * 512:(b + 1) * 512].rearrange("p (h k) -> p h k", h=HB)
                e_sn.done(eng.tensor_tensor(part, part, s_rec[:, hs].unsqueeze(2).broadcast_to((P, HB, P)), ALU.mult))
            for c in range(NB // 2, NB):
                dequantise(eng, "o", c, e_deq)
            e_bo.wait(eng, 0, 1)
            chain(eng.tensor_tensor(x1[:, :], x1[:, :], bo_row[:, :], ALU.add))
            e_sf.wait(eng, 0, 1)
            e_x2.done(eng.tensor_tensor(x2[:, :], ps_pj[0][:, :], x1[:, :], ALU.add))
            e_x2.wait(eng, 0, 1)

            layernorm(x3[:, :], x2[:, :], e_ln)
            split_low(eng, 0, 0, slice(LC, DC), e_elast)
            e_x3hi.wait(eng, 0, 1)
            e_x3lo.done(eng.tensor_tensor(x3t_lo[:, :], ps_t[:, :], x3t_hi[:, :].bitcast(F32), ALU.subtract))
            e_gate.wait(eng, 0, 2)
            e_tri.wait(eng, 0, 1)
            e_lge.wait(eng, 0, 1)
            chain(eng.tensor_scalar(score, score, 1.0, None, ALU.add))
            chain(eng.reciprocal(score, score))
            chain(eng.tensor_tensor(sc, score, gate_b[:, :], ALU.add))
            for i in range(NGRP):
                chain(eng.max(top8[:, i, :], sc[:, i * GE:(i + 1) * GE]))
            chain(eng.tensor_tensor(gs, top8[:, :, 0], top8[:, :, 1], ALU.add))

            def ranks(dst, v, n):
                other = v.unsqueeze(1).broadcast_to((P, n, n))
                own = v.unsqueeze(2).broadcast_to((P, n, n))
                a, b = cmp_a[:, 0:n, 0:n], cmp_b[:, 0:n, 0:n]
                chain(eng.tensor_tensor(a, other, own, ALU.is_gt))
                chain(eng.tensor_tensor(b, other, own, ALU.is_equal))
                chain(eng.tensor_tensor(b, b, earlier[:, 0:n, 0:n], ALU.mult))
                chain(eng.tensor_tensor(a, a, b, ALU.add))
                chain(eng.tensor_reduce(dst, a, AX.X, ALU.add))

            ranks(grank, gs, NGRP)
            chain(eng.tensor_scalar(gmask, grank, float(TOPG), None, ALU.is_lt))
            chain(eng.tensor_tensor(tmp.rearrange("p (g e) -> p g e", g=NGRP), sc.rearrange("p (g e) -> p g e", g=NGRP),
                                    gmask.unsqueeze(2).broadcast_to((P, NGRP, GE)), ALU.mult))
            split_low(eng, 0, 1, slice(LC, DC), e_elast)
            ranks(rank, tmp, NE)
            chain(eng.tensor_scalar(sel, rank, float(TOPK), None, ALU.is_lt))
            chain(eng.tensor_tensor(gw, score, sel, ALU.mult))
            chain(eng.tensor_reduce(wsum, gw, AX.X, ALU.add))
            chain(eng.tensor_scalar(wsum, wsum, 1e-20, None, ALU.add))
            chain(eng.reciprocal(wrec, wsum))
            e_gw.done(eng.tensor_scalar(gw, gw, wrec, RSCALE, ALU.mult, ALU.mult))
            e_gw.wait(eng, 0, 1)

            def shared_hidden(i):
                if i == 0:
                    e_sge.wait(eng, 0, 1)
                    chain(eng.tensor_scalar(sh_e[:, :], sh_e[:, :], 1.0, None, ALU.add))
                if i < DC:
                    part = slice(i * FS // DC, (i + 1) * FS // DC)
                    chain(eng.reciprocal(sh_e[:, part], sh_e[:, part]))
                if i == DC:
                    chain(eng.tensor_tensor(sh_a[:, :], ps_sg[:, :], sh_e[:, :], ALU.mult))
                if i == DC + 1:
                    e_sg.wait(eng, 0, 2)
                    e_shh.done(eng.tensor_tensor(sh_h[:, :], ps_su[:, :], sh_a[:, :], ALU.mult))

            def one_round(k, n):
                e_gc.done(eng.tensor_copy(g_col[:, :], gw[:, k * NR:(k + 1) * NR] if isinstance(k, int) else gw[:, bass.ds(k * NR, NR)]))
                e_gc.wait(eng, k, 1)
                for i in range(NR):
                    m = m_e[i % 2][:, :]
                    e_he.wait(eng, k, i + 1)
                    e_m1.done(eng.tensor_scalar(m, m, 1.0, None, ALU.add))
                    e_m1.wait(eng, k, i + 1)
                    e_m2.done(eng.reciprocal(m, m))
                    e_m2.wait(eng, k, i + 1)
                    e_m3.done(eng.scalar_tensor_tensor(m, ps_h[i % 2][:, 0:NF], g_col[:, i:i + 1], m, ALU.mult, ALU.mult))
                    e_m3.wait(eng, k, i + 1)
                    e_hid.done(eng.tensor_tensor(m_h[i % 2][:, :], ps_h[i % 2][:, NF:2 * NF], m, ALU.mult))
                    if i < n:
                        split_low(eng, k, i + 2, slice(LC, DC), e_elast)
                    if n < NR:
                        shared_hidden(i)

            rounds_of_experts(eng, one_round)
            e_yd.wait(eng, 0, 1)
            e_fin.done(eng.tensor_tensor(y_out[:, :], ps_y[:, :], x2[:, :], ALU.add))

        @block.tensor
        def _(eng):
            def transposes(dst, src):
                for c in range(4):
                    last = eng.transpose(dst[:, c * P:(c + 1) * P], src[:, c * P:(c + 1) * P], ident[:, :])
                return last

            def split_product(dst, a, b, lo, hi):
                steps = [(x, y) for (a_hi, a_lo), (b_hi, b_lo) in zip(a, b) for x, y in ((a_hi, b_hi), (a_hi, b_lo), (a_lo, b_hi))]
                for k in range(lo, hi):
                    last = eng.matmul(dst, *steps[k], start=(k == 0), stop=(k == len(steps) - 1))
                return last

            e_pool.wait(eng, 0, 2)

            def project_queries():
                e_lnxc.wait(eng, 0, 1)
                e_wq.wait(eng, 0, 1)
                for c in range(DC):
                    last = eng.matmul(ps_s[0][:, :], ln_xt[:, c * P:(c + 1) * P], wq[:, c, :], start=(c == 0), stop=(c == DC - 1))
                e_qp.done(last)

            def transpose_queries():
                for i in range(2):
                    e_qh.wait(eng, 0, i + 1)
                    e_qt.done(transposes(ps_pt[i], qf[i]))

            def step(eng, s, par, loop=False):
                proj, score, end = parts(s, loop)
                g = s - 1
                wi = 0 if (not loop and s == 0) else 2
                qi = 0 if (not loop and s == 1) else 1

                def products_of_queries(h):
                    if h == 0:
                        e_stk.wait(eng, g, 1)
                    if late:
                        e_qlo.wait(eng, 0, 2 * HC)
                    if loop or g > 0 or h >= NS:
                        e_exp.wait(eng, g, h + 1 - NS)
                    e_qk.done(eng.matmul(ps_s[h % NS][:, :], q_st[qi][0:NST * HD, h, :], stk[1 - par][0:NST * HD, h, :],
                                         start=True, stop=True))

                for h in range(NH):
                    late = not loop and s == 1 and h == 0
                    if score and not late:
                        products_of_queries(h)
                    if not loop and s <= 1 and h in (0, 8):
                        e_wlo.wait(eng, 0, 2 * s + 1 + h // 8)
                    if not loop and s == 1 and h == 2:
                        e_pz.wait(eng, 0, 1)
                    if proj:
                        u, half = divmod(h, 2)
                        i, j = divmod(u, GT)
                        if half == 0:
                            if i == 0:
                                e_clo.wait(eng, s, j + 1)
                            if u >= 2 + GT:
                                e_v.wait(eng, s, u - 1 - GT)
                            elif u >= 2:
                                e_kb.wait(eng, s, u - 1)
                            elif loop or s > 0:
                                e_v.wait(eng, s, u - 1)
                        part = slice(j * P, (j + 1) * P)
                        halves = [(cx_hi[:, k, part], cx_lo[:, k, part]) for k in range(DC)]
                        w = [(w_hi[wi + i][:, k, :], w_lo[wi + i][:, k, :]) for k in range(DC)]
                        n = 3 * DC // 2
                        if loop or s > 0 or j * P < IMG:
                            last = split_product(ps_a[u % 2][:, :], halves, w, half * n, (half + 1) * n)
                        elif half:
                            last = eng.matmul(ps_a[u % 2][:, :], halves[0][0], w[0][0], start=True, stop=True)
                        if half:
                            (e_kp, e_vp)[i].done(last)
                    if late:
                        products_of_queries(h)
                    gp, hp = (g, h - 2) if h >= 2 else (g - 1, h - 2 + NH)
                    if (score and h >= 2) or (end and h < 2):
                        e_exp.wait(eng, gp, hp + 1)
                        if loop or s >= 2 or h > 3:
                            e_pte.wait(eng, gp, hp - 1)
                        e_pt.done(transposes(ps_pt[hp % 2], p_sb[hp % NP]))
                    j = h // 2 - 2
                    if proj and h % 2 == 0 and 0 <= j < GT:
                        e_kn.wait(eng, s, j + 1)
                        if j == 0 and (loop or s > 2):
                            e_oadd.wait(eng, s - 2, 0)
                        if loop or s > 0 or j > 0:
                            e_klo.wait(eng, s, j)
                        e_kt.done(transposes(ps_t, kb[j % 2]))
                    gp, hp = (g, h - 4) if h >= 4 else (g - 1, h - 4 + NH)
                    if hp % HC == HC - 1 and ((score and h >= 4) or (end and h < 4)):
                        e_pte.wait(eng, gp, hp + 1)
                        if hp == HC - 1:
                            e_v.wait(eng, g, GT)
                            if loop or g > 0:
                                e_oc.wait(eng, g, 0)
                        c = hp // HC
                        vb = v_sb[1 - par] if h >= 4 else v_sb[par]
                        for k in range(GT):
                            for jp in range(HC):
                                head = c * HC + jp
                                last = eng.matmul(ps_o[jp * HD:(jp + 1) * HD, c * P:(c + 1) * P],
                                                  vb[:, k, head * HD:(head + 1) * HD],
                                                  pt_sb[head % NPT][:, k * P:(k + 1) * P],
                                                  start=(k == 0), stop=(k == GT - 1))
                        e_pv.done(last)
                    if end and h == 12:
                        e_oc.wait(eng, s - 2, 1)
                        if proj:
                            e_klo.wait(eng, s, GT)
                        e_ot.done(transposes(ps_t, ot_sb))
                    if not loop and s == 0 and h == 1:
                        e_lnx.wait(eng, 0, 1)
                        e_lnxt.done(transposes(ps_o, ln_x))
                    if not loop and s == 0 and h == 4:
                        project_queries()
                    if not loop and s == 0 and h == 10:
                        transpose_queries()

            steps(eng, step)
            e_osum.wait(eng, 0, 1)
            e_at.done(transposes(ps_t, o_st[0]))
            e_atc.wait(eng, 0, 1)
            e_wo.wait(eng, 0, 1)
            for c in range(DC):
                last = eng.matmul(ps_a[0][:, :], xnt[:, c * P:(c + 1) * P], wo[:, c, :], start=(c == 0), stop=(c == DC - 1))
            e_ap.done(last)

            e_ln.wait(eng, 0, 1)
            e_lnt.done(transposes(ps_t, yn))
            e_lntc.wait(eng, 0, 1)

            def project(n):
                i = QKV.index(n)
                e_deqp.wait(eng, 0, min(DC * (i + 1), NPOOL))
                if DC * (i + 1) > NPOOL:
                    e_deq.wait(eng, 0, DC * (i + 1) - NPOOL)
                for b in range(NB):
                    if NB * i + b >= 2:
                        e_pjb.wait(eng, 0, NB * i + b - 1)
                    for c in range(DC):
                        last = eng.matmul(ps_pj[b % 2][:, :], ynt[:, c * P:(c + 1) * P],
                                          codes[n][:, c, b * 512:(b + 1) * 512], start=(c == 0), stop=(c == DC - 1))
                    e_pj.done(last)

            def transpose_heads(n, first):
                for b in range(NB):
                    e_pjb.wait(eng, 0, NB * QKV.index(n) + b + 1)
                    if first + b >= 2:
                        e_trc.wait(eng, 0, first + b - 1)
                    e_tr.done(transposes(ps_tr[b % 2], qkv[n][:, b * 512:(b + 1) * 512]))

            project("q")
            project("v")
            transpose_heads("q", 0)
            project("k")
            transpose_heads("k", NB)
            e_trc.wait(eng, 0, 2 * NB)
            for b in range(NB):
                for h in range(b * HB, (b + 1) * HB):
                    part = slice(h * P, (h + 1) * P)
                    last = eng.matmul(ps_sc[b][:, (h % HB) * P:(h % HB + 1) * P], sqt[:, part], skt[:, part], start=True, stop=True)
                e_ss.done(last)
            for b in range(NB + 1):
                if b < NB:
                    e_sn.wait(eng, 0, b + 1)
                    if b >= 2:
                        e_sptc.wait(eng, 0, b - 1)
                    e_spt.done(transposes(ps_tr[b % 2], sp[:, b * 512:(b + 1) * 512]))
                if b:
                    e_sptc.wait(eng, 0, b)
                    for h in range((b - 1) * HB, b * HB):
                        part = slice(h * P, (h + 1) * P)
                        last = eng.matmul(ps_sc[b - 1][:, (h % HB) * P:(h % HB + 1) * P], sv[:, part], spt[:, part], start=True, stop=True)
                    e_so.done(last)
            e_soc.wait(eng, 0, NB)
            e_deq.wait(eng, 0, 3 * DC + NB - NPOOL)
            for h in range(SH):
                last = eng.matmul(ps_pj[0][:, :], sot[:, h * P:(h + 1) * P], codes_o[:, h, :], start=(h == 0), stop=(h == SH - 1))
            e_sf.done(last)

            e_ln.wait(eng, 0, 2)
            e_lnt.done(transposes(ps_t, x3))
            e_lntc.wait(eng, 0, 2)
            e_gate.wait(eng, 0, 2)

            def times_x3(dst, w):
                for c in range(DC):
                    last = eng.matmul(dst, x3t[:, c * P:(c + 1) * P], w[:, c, :], start=(c == 0), stop=(c == DC - 1))
                return last

            e_lg.done(times_x3(ps_lg[:, 0:NE], gate_w))
            e_shw.wait(eng, 0, 3)
            e_sg.done(times_x3(ps_sg[:, :], sh_w[0]))
            e_sg.done(times_x3(ps_su[:, :], sh_w[1]))
            def shared_down(c):
                eng.matmul(ps_y[:, :], sh_ht[:, c * P:(c + 1) * P], sh_w[2][:, c, :], start=False, stop=False,
                           skip_group_check=True)

            def expert_up(k, i):
                if not isinstance(k, int) or k * NR + i > 1:
                    e_hid.wait(eng, k, i - 1)
                e_ehi.wait(eng, k, i + 1)
                w_hi, w_lo = w13_hi[i % 2], w13_lo[i % 2]
                for c in range(DC):
                    for x in (x3t_hi, x3t_lo):
                        eng.matmul(ps_h[i % 2][:, :], x[:, c * P:(c + 1) * P], w_hi[:, c, :], start=(c == 0 and x is x3t_hi),
                                   stop=False)
                e_elo.wait(eng, k, i + 1)
                e_elast.wait(eng, k, i + 1)
                for c in range(DC):
                    last = eng.matmul(ps_h[i % 2][:, :], x3t_hi[:, c * P:(c + 1) * P], w_lo[:, c, :], start=False, stop=(c == DC - 1))
                e_h.done(last)

            def expert_transpose(k, i):
                e_hid.wait(eng, k, i + 1)
                for c in range(NF // P):
                    last = eng.transpose(ps_ht[i % 2][:, c * P:(c + 1) * P], m_h[i % 2][:, c * P:(c + 1) * P], ident[:, :])
                e_ht.done(last)

            def expert_down(k, i, begin=False, end=None):
                e_htc.wait(eng, k, i + 1)
                for c in range(NF // P):
                    last = eng.matmul(ps_y[:, :], m_ht[i % 2][:, c * P:(c + 1) * P], w2[i % NR][:, c, :], start=(begin and c == 0),
                                      stop=(end is not None and c == NF // P - 1), skip_group_check=True)
                (end or e_y).done(last)

            def experts(k, first=False, final=False):
                for i in range(NR):
                    if not (final and i == NR - 1) and not (first and i == 0):
                        expert_up(k, i + 1)
                    if not (first and i == 0):
                        expert_down(k, i - 1, begin=(first and i == 1))
                    if final and i == NR - 1:
                        e_shtc.wait(eng, 0, 1)
                        for c in range(DC):
                            shared_down(c)
                    expert_transpose(k, i)
                    if final and i == SHARED_SLOT:
                        e_shh.wait(eng, 0, 1)
                        e_sht.done(transposes(ps_lg, sh_h))

            e_x3lo.wait(eng, 0, 1)
            expert_up(0, 0)
            expert_up(0, 1)
            experts(0, first=True)
            with eng.Fori(1, NE // NR - 1) as k:
                experts(k)
            experts(NE // NR - 1, final=True)
            expert_down(NE // NR - 1, NR - 1, end=e_yd)


NAMES = ["q_b", "k_b", "v_b", "k_img_b", "v_img_b", "o_b", "norm_q_w", "norm_k_w", "norm_k_img_w"]


def kernel(**inputs):
    import numpy as np
    import concourse.bacc as bacc
    from concourse import mybir as mb
    from concourse.bass_utils import run_bass_kernel_spmd as run

    def lay(a):
        return np.ascontiguousarray(np.asarray(a))

    arrays = {"x": lay(inputs["x"][0]), "ctx_t": lay(np.asarray(inputs["ctx_2048"])[0].T)}
    for n in NAMES:
        arrays[n] = lay(inputs["L0_xattn_" + n])
    for n in ["q", "k", "v", "k_img", "v_img", "o"]:
        arrays[n + "_wt"] = lay(np.asarray(inputs[f"L0_xattn_{n}_w"]).T)
    for n in "qkvo":
        for part in ("codes", "scales"):
            arrays[f"w{n}_{part}"] = lay(inputs[f"L0_attn_w{n}_{part}"])
        arrays["b" + n] = lay(inputs["L0_attn_b" + n])
    for n in ("w1", "w2", "w3", "gate_bias", "shared_gate", "shared_up", "shared_down"):
        arrays[n] = lay(inputs["L0_ffn_" + n])
    arrays["gate_wt"] = lay(np.asarray(inputs["L0_ffn_gate_w"]).T)
    nc = bacc.Bacc("TRN2", target_bir_lowering=False, num_devices=1)
    t = {n: nc.dram_tensor(n, a.shape, mb.dt.from_np(a.dtype), kind="ExternalInput").ap() for n, a in arrays.items()}
    out = nc.dram_tensor("out", (P, D), mb.dt.float32, kind="ExternalOutput").ap()
    program(nc, t, out)
    r = run(nc, [arrays], core_ids=[0])
    return r.results[0]["out"].reshape(1, P, D)
```
